# Optimizing a Trainium2 kernel written in Bass

```python
import numpy as np
import jax
import jax.numpy as jnp

def _softmax(x, axis=-1):
    return jax.nn.softmax(x, axis=axis)

def _gelu(x):
    return jax.nn.gelu(x, approximate=True)

def _silu(x):
    return jax.nn.silu(x)

def _sigmoid(x):
    return jax.nn.sigmoid(x)

def _layernorm(x, axis=-1, eps=1e-05):
    m = jnp.mean(x, axis=axis, keepdims=True)
    v = jnp.var(x, axis=axis, keepdims=True)
    return (x - m) / jnp.sqrt(v + eps)

def _scatter_add(tgt, idx, src, axis=0):
    return tgt.at[idx].add(src)

def _segment_sum(src, seg, n):
    return jax.ops.segment_sum(src, seg, n)
kernel_name = 'mk_gnn_resnorm_d2_gnn_r8_b382b8'

def setup_inputs(seed: int=0):
    np.random.seed(seed)
    _w = jnp.asarray

    def _rec_inputs():
        import jax
        import jax.numpy as jnp
        _gk = jax.random.key(seed)
        x = -0.0005121 + 1.001 * jax.random.normal(jax.random.fold_in(_gk, 1), (12500, 64), jnp.float32)
        _s = jax.random.randint(jax.random.fold_in(_gk, 2), (100000,), 0, 12500, jnp.int32)
        _d = jax.random.randint(jax.random.fold_in(_gk, 3), (100000,), 0, 12500, jnp.int32)
        _loop = jnp.arange(12500, dtype=jnp.int32)
        src = jnp.concatenate([_s, _d, _loop])
        dst = jnp.concatenate([_d, _s, _loop])
        _o = jnp.argsort(dst, stable=True)
        src = src[_o]
        dst = dst[_o]
        edge_attr_16 = 0.000254156 + 0.999948 * jax.random.normal(jax.random.fold_in(_gk, 12), (212500, 16), jnp.float32)
        return (x, src, dst, edge_attr_16)
    x, src, dst, edge_attr_16 = _rec_inputs()

    def _L0_gnn_setup():
        import jax, jax.numpy as jnp
        import numpy as np
        N_NODES = 6250
        N_EDGES = 200000
        D_FEAT = 64
        NEG_SLOPE = 0.2
        key = jax.random.key(seed)
        k1, k2, k3, k4, k5 = jax.random.split(key, 5)
        z = jax.random.normal(k1, (N_NODES, D_FEAT), dtype=jnp.float32)
        attn_l = jax.random.normal(k2, (D_FEAT,), dtype=jnp.float32) * 0.1
        attn_r = jax.random.normal(k3, (D_FEAT,), dtype=jnp.float32) * 0.1
        src = jax.random.randint(k4, (N_EDGES,), 0, N_NODES, dtype=jnp.int32)
        dst = jax.random.randint(k5, (N_EDGES,), 0, N_NODES, dtype=jnp.int32)
        return {'z': z, 'attn_l': attn_l, 'attn_r': attn_r, 'src': src, 'dst': dst}
    _L0_gnn_all = _L0_gnn_setup()
    _L0_gnn_in = {k: v for k, v in _L0_gnn_all.items() if k in ('attn_l', 'attn_r')}
    del _L0_gnn_all

    def _L1_gnn_setup():
        import jax, jax.numpy as jnp
        import numpy as np
        N = 6250
        E = 100000
        D = 64
        EDGE_DIM = 16
        L = 3
        MSG_IN = 2 * D + EDGE_DIM
        UPD_IN = D + D
        key = jax.random.key(seed)
        ks = jax.random.split(key, 8)
        x = jax.random.normal(ks[0], (N, D), dtype=jnp.float32)
        edge_index = jax.random.randint(ks[1], (2, E), 0, N, dtype=jnp.int64)
        edge_attr = jax.random.normal(ks[2], (E, EDGE_DIM), dtype=jnp.float32)
        sc_m = 1.0 / np.sqrt(MSG_IN)
        sc_u = 1.0 / np.sqrt(UPD_IN)
        msg_w = jax.random.uniform(ks[3], (L, MSG_IN, D), jnp.float32, -sc_m, sc_m)
        msg_b = jax.random.uniform(ks[4], (L, D), jnp.float32, -sc_m, sc_m)
        upd_w = jax.random.uniform(ks[5], (L, UPD_IN, D), jnp.float32, -sc_u, sc_u)
        upd_b = jax.random.uniform(ks[6], (L, D), jnp.float32, -sc_u, sc_u)
        return {'x': x, 'edge_index': edge_index, 'edge_attr': edge_attr, 'msg_w': msg_w, 'msg_b': msg_b, 'upd_w': upd_w, 'upd_b': upd_b}
    _L1_gnn_all = _L1_gnn_setup()
    _L1_gnn_in = {k: v for k, v in _L1_gnn_all.items() if k in ('msg_w', 'msg_b', 'upd_w', 'upd_b')}
    del _L1_gnn_all
    return {'x': x, 'src': src, 'dst': dst, 'edge_attr_16': edge_attr_16, 'L0_gnn_attn_l': _L0_gnn_in['attn_l'], 'L0_gnn_attn_r': _L0_gnn_in['attn_r'], 'L1_gnn_msg_w': _L1_gnn_in['msg_w'], 'L1_gnn_msg_b': _L1_gnn_in['msg_b'], 'L1_gnn_upd_w': _L1_gnn_in['upd_w'], 'L1_gnn_upd_b': _L1_gnn_in['upd_b']}

def reference(x, src, dst, edge_attr_16, L0_gnn_attn_l, L0_gnn_attn_r, L1_gnn_msg_w, L1_gnn_msg_b, L1_gnn_upd_w, L1_gnn_upd_b):
    import jax
    import jax.numpy as jnp

    def _L0_gnn_ref(z, attn_l, attn_r, src, dst):
        import jax, jax.numpy as jnp
        import numpy as np
        N_NODES = 6250
        N_EDGES = 200000
        D_FEAT = 64
        NEG_SLOPE = 0.2
        n = z.shape[0]
        el = z @ attn_l
        er = z @ attn_r
        e = jax.nn.leaky_relu(el[src] + er[dst], negative_slope=NEG_SLOPE)
        m = jax.ops.segment_max(e, dst, num_segments=n)
        ex = jnp.exp(e - m[dst])
        den = jax.ops.segment_sum(ex, dst, num_segments=n)
        a = ex / den[dst]
        msg = z[src] * a[:, None]
        rst = jax.ops.segment_sum(msg, dst, num_segments=n)
        return jax.nn.elu(rst)

    def _L1_gnn_ref(x, edge_index, edge_attr, msg_w, msg_b, upd_w, upd_b):
        import jax, jax.numpy as jnp
        import numpy as np
        N = 6250
        E = 100000
        D = 64
        EDGE_DIM = 16
        L = 3
        MSG_IN = 2 * D + EDGE_DIM
        UPD_IN = D + D
        src = edge_index[0]
        dst = edge_index[1]
        n = x.shape[0]
        num_layers = msg_w.shape[0]
        for l in range(num_layers):
            x_i = x[dst]
            x_j = x[src]
            m_in = jnp.concatenate([x_i, x_j, edge_attr], axis=1)
            m = jax.nn.relu(m_in @ msg_w[l] + msg_b[l])
            agg = jax.ops.segment_sum(m, dst, num_segments=n)
            u_in = jnp.concatenate([x, agg], axis=1)
            x = jax.nn.relu(u_in @ upd_w[l] + upd_b[l])
        return x
    edge_index = jnp.stack([src, dst])
    x = _layernorm(x + _L0_gnn_ref(x, L0_gnn_attn_l, L0_gnn_attn_r, src, dst), axis=-1)
    x = _layernorm(x + _L1_gnn_ref(x, edge_index, edge_attr_16, L1_gnn_msg_w, L1_gnn_msg_b, L1_gnn_upd_w, L1_gnn_upd_b), axis=-1)
    return x

_drawn_inputs = setup_inputs


def setup_inputs(seed=0):
    import zlib

    import numpy as np

    out = dict(_drawn_inputs(seed))
    spreads = {}
    factors = {'L0_gnn_attn_r': 3.007}
    for name, (base, spread) in spreads.items():
        noise = np.random.default_rng([zlib.crc32(name.encode()), seed]).standard_normal(out[name].shape)
        drawn = base * np.exp(spread * noise) if base else spread * noise
        out[name] = jnp.asarray(drawn.astype(out[name].dtype))
    for name, factor in factors.items():
        out[name] = (out[name] * factor).astype(out[name].dtype)
    return out
```

```python
from contextlib import ExitStack

import numpy as np

import concourse.bass as bass
from concourse import mybir
from concourse.bass import IndirectOffsetOnAxis

F32 = mybir.dt.float32
BF16 = mybir.dt.bfloat16
I32 = mybir.dt.int32
ALU = mybir.AluOpType
ACT = mybir.ActivationFunctionType
AX = mybir.AxisListType

N, D = 12500, 64
E, DE = 212500, 16
LAYERS = 3
PART = 128
K = 16
H = K // 2
TILES = -(-E // (2 * K * PART)) * 2 * K
ITERS = TILES // (2 * K)
NB = -(-N // PART)
GB = 4
GU = 5
GI = -(-NB // (GB * GU))
NBP = GI * GU * GB
NT = NB - 1
NREST = N - NT * PART
BIG = 2.0 ** 126
EPS = 1e-5
SLOPE = 0.2
CW = 2 * D
DEN = D - 1
PW = 3 * D


class Chain:

    def __init__(self, engine, sem, base=0):
        self.engine, self.sem, self.base, self.n = engine, sem, base, 0

    def link(self, ins):
        self.n += 1
        ins.then_inc(self.sem, 1)
        self.engine.wait_ge(self.sem, self.base + self.n)


def build(nc, x, src_cols, dst_cols, dst_flat, dst_first, dst_last, edge_t, attn_l, attn_r,
          w_ij, w_e, w_u, b_ij, b_u, out):
    ds = bass.ds
    ctx = ExitStack()
    with ctx:
        def sb(name, shape, dt=F32):
            return ctx.enter_context(nc.sbuf_tensor(name, shape, dt))

        def sem(name):
            return ctx.enter_context(nc.semaphore(name))

        q_table = nc.dram_tensor("q_table", (NBP * PART, D), F32).ap()

        cat = sb("cat", [PART, NBP, CW])
        p3_raw = sb("p3_raw", [PART, max(NBP * PW // 2, 4 * TILES)])
        p3 = p3_raw[:, :].bitcast(BF16)
        xn = sb("xn", [PART, NBP, D])
        rows = sb("rows", [PART, 2, K, D])
        hot = sb("hot", [PART, 2 * K, 2 * PART])
        hot_t = sb("hot_t", [PART, 2, 2, 2 * PART], BF16)
        weighted = sb("weighted", [PART, 2, K, D + 1])
        rel = sb("rel", [PART, TILES])
        relc = sb("relc", [PART, 2, K])
        idx = sb("idx", [PART, 2, K], I32)
        edge_f = sb("edge_f", [PART, 2, 4, PART])
        block_row = sb("block_row", [1, TILES], I32)
        iota_i = sb("iota_i", [PART, 2 * PART], I32)
        iota = sb("iota", [PART, 2 * PART])
        pidx_i = sb("pidx_i", [PART, 1], I32)
        pidx = sb("pidx", [PART, 1])
        ident = sb("ident", [PART, PART])
        ones = sb("ones", [1, PART])
        zeros = sb("zeros", [PART, GB, D])
        eps = sb("eps", [PART, 1])
        al = sb("al", [PART, D])
        ar = sb("ar", [PART, D])
        er = sb("er", [PART, NBP])
        er_rest = sb("er_rest", [PART, NBP])
        er3 = sb("er3", [PART, NBP, 3], BF16)
        x_t = sb("x_t", [D, GU, GB * PART])
        w_ij_sb = sb("w_ij_sb", [D, 2 * D])
        w_e_sb = sb("w_e_sb", [PART, D])
        w_u_sb = sb("w_u_sb", [CW, D])
        b_ij_sb = sb("b_ij_sb", [1, 2 * D])
        b_u_sb = sb("b_u_sb", [1, D])
        p_rest = sb("p_rest", [PART, GB, D])
        el = sb("el", [PART, K])
        ere = sb("ere", [PART, K])
        ec = sb("ec", [PART, K])
        e_row = sb("e_row", [K, PART])
        dst_row = sb("dst_row", [K, 2, PART + 2], I32)
        same = sb("same", [K, PART + 1])
        fwd = sb("fwd", [K, PART])
        bwd = sb("bwd", [K, PART])
        ends_row = sb("ends_row", [1, 2 * K])
        fwd_chain = sb("fwd_chain", [1, 2, K + 1])
        bwd_chain = sb("bwd_chain", [1, K + 1])
        carry_row = sb("carry_row", [1, 2 * K])
        carry_col = sb("carry_col", [K, 2])
        shift = sb("shift", [K, PART])
        w_row = sb("w_row", [K, PART])
        w_col = sb("w_col", [PART, K])
        resc = sb("resc", [1, 2])
        first_hot = sb("first_hot", [PART, 2])
        resc_col = sb("resc_col", [PART, 1])
        stat = sb("stat", [PART, 4, NB])

        flags = p3[0:1, 0:4 * (TILES + 1)].rearrange("p (f t) -> p f t", f=4)
        stage = hot[:, :, :].rearrange("p a b -> p (a b)")
        el_prod = p3_raw[:, -K * D:].rearrange("p (t d) -> p t d", d=D)
        big_y = stage[:, 0:NB * D].rearrange("p (b d) -> p b d", d=D)
        big_z = p3_raw[:, 0:NB * D].rearrange("p (b d) -> p b d", d=D)
        n_stage = GU * GB * CW
        stage_u = stage[:, 0:n_stage].rearrange("p (u b d) -> p u b d", u=GU, b=GB)
        stage_ut = stage[:, n_stage:2 * n_stage].rearrange("p (u b n) -> p u b n", u=GU, b=GB)
        stage_x = stage[:, 0:n_stage // 2].rearrange("p (u b d) -> p u b d", u=GU, b=GB)
        stage_pq = stage[:, n_stage:2 * n_stage].rearrange("p (u b d) -> p u b d", u=GU, b=GB)
        ints = stage.bitcast(I32)
        dst_c_i = ints[:, 0:TILES]
        first_b_i = ints[:, TILES:2 * TILES]
        first_i = ints[0:1, 2 * TILES:3 * TILES]
        last_i = ints[0:1, 3 * TILES:4 * TILES]

        ps = ctx.enter_context(nc.psum_tensor("ps", [PART, 8, 512], F32))

        def t_bank(pair):
            return ps[:, pair % 2, :]

        def pre_bank(half):
            return ps[:, 2 + half % 2, :].rearrange("p (t d) -> p t d", d=D)

        def agg_slot(tile):
            return ps[:, 4 + tile % 4 // 2, 256 * (tile % 2):256 * (tile % 2) + 256].rearrange(
                "p (j d) -> p j d", j=2)

        def er_bank(b):
            return ps[:, 2 + b, 0:3 * K].rearrange("p (t s) -> p t s", s=3)

        def misc(b):
            m = ps[:, 6 + b, :]
            return {"e_t": m[0:K, 0:PART], "ends": m[0:1, 128:128 + 2 * K], "carry": m[0:K, 160:162],
                    "w_t": m[:, 192:192 + K], "resc": m[:, 224:225]}

        s_in = sem("s_in")
        s_iota = sem("s_iota")
        s_const = sem("s_const")
        s_pro = sem("s_pro")
        s_idx = [sem(f"s_idx{b}") for b in range(2)]
        s_dstrow = [sem(f"s_dstrow{b}") for b in range(2)]
        s_rows0 = [[sem(f"s_rows0_{b}{h}") for h in range(2)] for b in range(2)]
        s_hot0 = sem("s_hot0")
        s_t0 = sem("s_t0")
        s_tc0 = sem("s_tc0")
        s_fh = sem("s_fh")
        s_er = sem("s_er")
        s_ec = sem("s_ec")
        s_et = sem("s_et")
        s_ends = sem("s_ends")
        s_endst = sem("s_endst")
        s_carry = sem("s_carry")
        s_carryt = sem("s_carryt")
        s_shift = sem("s_shift")
        s_diff = sem("s_diff")
        s_w = sem("s_w")
        s_resc = sem("s_resc")
        s_rescm = sem("s_rescm")
        s_wt = sem("s_wt")
        s_weighted = sem("s_weighted")
        s_aggm0 = sem("s_aggm0")
        s_acc0 = [sem(f"s_acc0_{b}") for b in range(2)]
        s_ch0 = sem("s_ch0")
        s_ln = sem("s_ln")
        s_lna = sem("s_lna")
        s_x1 = sem("s_x1")
        s_w_in = sem("s_w_in")
        s_xs = sem("s_xs")
        s_xt = sem("s_xt")
        s_xtc = sem("s_xtc")
        s_pq = sem("s_pq")
        s_split = sem("s_split")
        s_p3 = sem("s_p3")
        s_qc = sem("s_qc")
        s_qt = [sem(f"s_qt{u}") for u in range(GU)]
        s_rows = [[sem(f"s_rows_{b}{h}") for h in range(2)] for b in range(2)]
        s_edge = [sem(f"s_edge{b}") for b in range(2)]
        s_relc = sem("s_relc")
        s_hot = sem("s_hot")
        s_t = sem("s_t")
        s_tc = sem("s_tc")
        s_pre = sem("s_pre")
        s_add = sem("s_add")
        s_relu = sem("s_relu")
        s_aggm = sem("s_aggm")
        s_acc = [[sem(f"s_acc_{b}{h}") for h in range(2)] for b in range(2)]
        s_us = sem("s_us")
        s_uz = sem("s_uz")
        s_ut = sem("s_ut")
        s_utc = sem("s_utc")
        s_up = sem("s_up")
        s_ux = sem("s_ux")
        s_out = sem("s_out")
        s_past = [sem(f"s_past_{e}") for e in ("pool", "pe", "dve")]
        block = ctx.enter_context(nc.Block())

        N_IN = 9
        CH0 = 42

        @block.sync
        def _(sp):
            sp.dma_start(dst_c_i, dst_cols).then_inc(s_in, 16)
            sp.dma_start(first_b_i, dst_first.partition_broadcast(PART)).then_inc(s_in, 16)
            sp.dma_start(first_i, dst_first).then_inc(s_in, 16)
            sp.dma_start(last_i, dst_last).then_inc(s_in, 16)
            sp.dma_start(al[:, :], attn_l.partition_broadcast(PART)).then_inc(s_in, 16)
            sp.dma_start(ar[:, :], attn_r.partition_broadcast(PART)).then_inc(s_in, 16)
            sp.dma_start(xn[:, 0:NT, :], x[0:NT * PART, :].rearrange("(b p) d -> p b d", p=PART)
                         ).then_inc(s_in, 16)
            sp.dma_start(xn[0:NREST, NT, :], x[NT * PART:N, :]).then_inc(s_in, 16)
            sp.dma_start(xn[NREST:PART, NT, :], x[0:PART - NREST, :]).then_inc(s_in, 16)

            with sp.Fori(0, ITERS) as i:
                for b in range(2):
                    for h in range(2):
                        sp.wait_ge(s_rows0[b][h], i * (16 * H))
                    sp.dma_start(idx[:, b, :], src_cols[:, ds((i * 2 + b) * K, K)]).then_inc(s_idx[b], 16)
                    sp.wait_ge(s_acc0[b], i * K)
                    sp.dma_start(dst_row[:, b, :], dst_rows(dst_flat, (i * 2 + b) * (K * PART))
                                 ).then_inc(s_dstrow[b], 16)

            with sp.Fori(0, LAYERS) as layer:
                sp.wait_ge(s_ux, layer * (GI * GU))
                sp.dma_start(w_ij_sb[:, :], w_ij[ds(layer * D, D), :]).then_inc(s_w_in, 16)
                sp.dma_start(w_e_sb[:, :], w_e[ds(layer * PART, PART), :]).then_inc(s_w_in, 16)
                sp.dma_start(w_u_sb[:, :], w_u[ds(layer * CW, CW), :]).then_inc(s_w_in, 16)
                sp.dma_start(b_ij_sb[:, :], b_ij[ds(layer, 1), :]).then_inc(s_w_in, 16)
                sp.dma_start(b_u_sb[:, :], b_u[ds(layer, 1), :]).then_inc(s_w_in, 16)
                with sp.Fori(0, GI) as i:
                    g = sp.snap(layer * GI + i)
                    for u in range(GU):
                        sp.wait_ge(s_qc, g * GU + (u + 1))
                        rows_q = q_table.rearrange("(b p) d -> p b d", p=PART)
                        sp.dma_start(rows_q[:, ds((i * GU + u) * GB, GB), :], stage_pq[:, u, :, D:2 * D]
                                     ).then_inc(s_qt[u], 16)
                with sp.Fori(0, ITERS) as i:
                    g = sp.snap(layer * ITERS + i)
                    for b in range(2):
                        for h in range(2):
                            sp.wait_ge(s_rows[b][h], g * (16 * H))
                        sp.dma_start(idx[:, b, :], src_cols[:, ds((i * 2 + b) * K, K)]).then_inc(s_idx[b], 16)
                        sp.wait_ge(s_acc[b][1], g * H)
                        for q in range(4):
                            sp.dma_start(edge_f[32 * q:32 * q + DE, b, :, :].rearrange("p t e -> p (t e)"),
                                         edge_t[:, ds((i * 2 + b) * (K * PART) + q * 4 * PART, 4 * PART)]
                                         ).then_inc(s_edge[b], 16)

            sp.wait_ge(s_x1, 2)
            sp.dma_start(out[0:NT * PART, :].rearrange("(b p) d -> p b d", p=PART), xn[:, 0:NT, :]
                         ).then_inc(s_out, 16)
            sp.dma_start(out[NT * PART:N, :], xn[0:NREST, NT, :]).then_inc(s_out, 16)
            sp.wait_ge(s_out, 32)

        @block.gpsimd
        def _(pool):
            nc.gpsimd.iota(iota_i[:, :], [[1, 2 * PART]], base=0, channel_multiplier=0)
            nc.gpsimd.iota(pidx_i[:, :], [[1, 1]], base=0, channel_multiplier=1).then_inc(s_iota, 1)

            def gather(table, b, h, s):
                for t in range(h * H, h * H + H):
                    nc.gpsimd.indirect_dma_start(
                        rows[:, b, t, :], None, table,
                        IndirectOffsetOnAxis(ap=idx[:, b, t:t + 1], axis=0)).then_inc(s, 16)

            with pool.Fori(0, ITERS) as i:
                for b in range(2):
                    loaded, used = pool.snap(i * 16 + 16), pool.snap(i * K)
                    pool.wait_ge(s_idx[b], loaded)
                    pool.wait_ge(s_acc0[b], used)
                    hold_waits(pool, s_past[0])
                    for h in range(2):
                        gather(x, b, h, s_rows0[b][h])
            with pool.Fori(0, LAYERS) as layer:
                for u in range(GU):
                    pool.wait_ge(s_qt[u], layer * (16 * GI) + 16 * GI)
                hold_waits(pool, s_past[0])
                with pool.Fori(0, ITERS) as i:
                    g = pool.snap(layer * ITERS + i)
                    loaded, used = pool.snap(g * 16 + (16 * ITERS + 16)), pool.snap(g * H)
                    for b in range(2):
                        for h in range(2):
                            if h == 0:
                                pool.wait_ge(s_idx[b], loaded)
                            pool.wait_ge(s_acc[b][h], used)
                            hold_waits(pool, s_past[0])
                            gather(q_table, b, h, s_rows[b][h])

        @block.scalar
        def _(act):
            act.wait_ge(s_const, 1)

            with act.Fori(0, ITERS) as i:
                i16 = act.snap(i * 16)
                i2 = act.snap(i * 2)

                def copy_pairs(b, lo, hi):
                    for p in range(8 * b + lo, 8 * b + hi):
                        act.wait_ge(s_t0, i16 + (p + 1))
                        if p >= 2:
                            act.wait_ge(s_er, i16 + (p - 1))
                        else:
                            act.wait_ge(s_er, i16)
                        if p % 8 == 0:
                            act.wait_ge(s_acc0[b], i16)
                            nc.scalar.copy(first_hot[:, b:b + 1], t_bank(p)[:, 0:1]).then_inc(s_fh, 1)
                        nc.scalar.copy(hot_t[:, p % 2, :, :].rearrange("p a b -> p (a b)"), t_bank(p)
                                       ).then_inc(s_tc0, 1)

                def exps(b):
                    act.wait_ge(s_shift, i2 + (b + 1))
                    nc.scalar.activation(w_row[:, :], shift[:, :], ACT.Exp).then_inc(s_w, 1)
                    act.wait_ge(s_diff, i2 + (b + 1))
                    nc.scalar.activation(resc[:, 1:2], resc[:, 0:1], ACT.Exp).then_inc(s_resc, 1)

                copy_pairs(0, 0, 8)
                copy_pairs(1, 0, 6)
                exps(0)
                copy_pairs(1, 6, 8)
                exps(1)

            def root(n):
                act.wait_ge(s_ln, n)
                nc.scalar.activation(stat[:, 2, :], stat[:, 1, :], ACT.Sqrt, bias=eps[:, :],
                                     scale=1.0 / D).then_inc(s_lna, 1)

            act.wait_ge(s_ln, 4)
            nc.scalar.activation(big_z, big_z, ACT.Exp).then_inc(s_lna, 1)
            root(11)

            with act.Fori(0, LAYERS) as layer:
                with act.Fori(0, GI) as i:
                    g = act.snap(layer * GI + i)
                    g5 = act.snap(g * GU)
                    g16 = act.snap(g * 16)

                    def copy_xt(u):
                        act.wait_ge(s_xt, g5 + (u + 1))
                        nc.scalar.copy(x_t[:, u, :], ps[0:D, u % 4, :]).then_inc(s_xtc, 1)

                    def copy_q(u):
                        act.wait_ge(s_pq, g5 + (u + 1))
                        act.wait_ge(s_qt[u], g16)
                        act.wait_ge(s_p3, g5)
                        nc.scalar.copy(stage_pq[:, u, :, :].rearrange("p b d -> p (b d)"), ps[:, 4 + u % 4, :]
                                       ).then_inc(s_qc, 1)
                    for u in range(4):
                        copy_xt(u)
                    copy_q(0)
                    copy_xt(4)
                    for u in range(1, GU):
                        copy_q(u)

                with act.Fori(0, ITERS) as i:
                    g = act.snap(layer * ITERS + i)
                    g16 = act.snap(g * 16)
                    g4 = act.snap(g * 4)
                    for q in range(4):
                        b, h = q // 2, q % 2
                        for p in range(4 * q, 4 * q + 4):
                            act.wait_ge(s_t, g16 + (p + 1))
                            if p >= 2:
                                act.wait_ge(s_pre, g16 + (p - 1))
                            nc.scalar.copy(hot_t[:, p % 2, :, :].rearrange("p a b -> p (a b)"), t_bank(p)
                                           ).then_inc(s_tc, 1)
                        act.wait_ge(s_add, g4 + (q + 1))
                        m = rows[:, b, h * H:h * H + H, :].rearrange("p t d -> p (t d)")
                        nc.scalar.activation(m, m, ACT.Relu).then_inc(s_relu, 1)

                with act.Fori(0, GI) as i:
                    g5 = act.snap((layer * GI + i) * GU)

                    def copy_ut(u):
                        act.wait_ge(s_ut, g5 + (u + 1))
                        nc.scalar.copy(stage_ut[:, u, :, :].rearrange("p b n -> p (b n)"), ps[:, u % 4, :]
                                       ).then_inc(s_utc, 1)

                    def relu_x(u):
                        act.wait_ge(s_up, g5 + (u + 1))
                        nc.scalar.activation(cat[:, ds((i * GU + u) * GB, GB), 0:D],
                                             ps[:, 4 + u % 4, 0:GB * D].rearrange("p (b d) -> p b d", d=D),
                                             ACT.Relu).then_inc(s_ux, 1)
                    for u in range(4):
                        copy_ut(u)
                    relu_x(0)
                    copy_ut(4)
                    for u in range(1, GU):
                        relu_x(u)
            root(19)

        @block.tensor
        def _(pe):
            regs = [pe.alloc_register(f"tile_block{k}") for k in range(K)]
            pe.wait_ge(s_const, 1)

            with pe.Fori(0, ITERS) as i:
                i32 = pe.snap(i * 32)
                i16 = pe.snap(i * 16)
                i2 = pe.snap(i * 2)

                def er_pairs(b, lo, hi):
                    at = load_blocks(pe, regs, block_row, (i * 2 + b) * K + 2 * lo, 2 * (hi - lo))
                    for p in range(8 * b + lo, 8 * b + hi):
                        pe.wait_ge(s_hot0, i32 + (2 * p + 2))
                        if p >= 2:
                            pe.wait_ge(s_tc0, i16 + (p - 1))
                        for tt in range(2):
                            for j in range(2):
                                last = nc.tensor.transpose(
                                    t_bank(p)[:, tt * 256 + j * PART:tt * 256 + (j + 1) * PART],
                                    hot[:, 2 * p + tt, j * PART:(j + 1) * PART], ident[:, :])
                        last.then_inc(s_t0, 1)
                        pe.wait_ge(s_tc0, i16 + (p + 1))
                        if p % 8 == 0:
                            pe.wait_ge(s_ec, i2 + (b - 1)) if b else pe.wait_ge(s_ec, i2)
                        for tt in range(2):
                            t = 2 * (p % 8) + tt
                            for j in range(2):
                                last = nc.tensor.matmul(er_bank(b)[:, t, :], hot_t[:, p % 2, tt, j * PART:(j + 1) * PART],
                                                        er3[:, :, :].rearrange("p b s -> p (b s)")[:, ds((at[t - 2 * lo] + j) * 3, 3)],
                                                        start=(j == 0), stop=(j == 1))
                        last.then_inc(s_er, 1)

                def row_e(b):
                    pe.wait_ge(s_ec, i2 + (b + 1))
                    nc.tensor.transpose(misc(b)["e_t"], ec[:, :], ident[:, :]).then_inc(s_et, 1)

                def row_ends(b):
                    pe.wait_ge(s_ends, i2 + (b + 1))
                    hold_waits(pe, s_past[1])
                    nc.tensor.transpose(misc(b)["ends"][:, 0:K], fwd[:, PART - 1:PART], ident[0:K, 0:K])
                    nc.tensor.transpose(misc(b)["ends"][:, K:2 * K], bwd[:, 0:1], ident[0:K, 0:K]
                                        ).then_inc(s_endst, 1)

                def col_carries(b):
                    pe.wait_ge(s_carry, i2 + (b + 1))
                    hold_waits(pe, s_past[1])
                    nc.tensor.transpose(misc(b)["carry"][:, 0:1], carry_row[:, 0:K], ident[0:1, 0:1])
                    nc.tensor.transpose(misc(b)["carry"][:, 1:2], carry_row[:, K:2 * K], ident[0:1, 0:1]
                                        ).then_inc(s_carryt, 1)

                def col_weights(b):
                    pe.wait_ge(s_w, i2 + (b + 1))
                    hold_waits(pe, s_past[1])
                    nc.tensor.transpose(misc(b)["w_t"], w_row[:, :], ident[0:K, 0:K])
                    pe.wait_ge(s_rescm, i2 + (b + 1))
                    nc.tensor.matmul(misc(b)["resc"], ones[:, :], resc[:, 0:1], start=True, stop=True
                                     ).then_inc(s_wt, 1)

                def sums(b, lo, hi):
                    if lo == 0:
                        pe.wait_ge(s_weighted, i2 + (b + 1))
                    for t in range(lo, hi):
                        tau = K * b + t
                        wait_slot(pe, s_acc0, i16, tau, K)
                        for j in range(2):
                            last = nc.tensor.matmul(agg_slot(tau)[:, j, 0:D + 1], hot[:, tau, j * PART:(j + 1) * PART],
                                                    weighted[:, b, t, :], start=True, stop=True)
                        last.then_inc(s_aggm0, 1)

                er_pairs(0, 0, 8)
                row_e(0)
                er_pairs(1, 0, 2)
                row_ends(0)
                er_pairs(1, 2, 4)
                col_carries(0)
                er_pairs(1, 4, 8)
                col_weights(0)
                sums(0, 0, 4)
                row_e(1)
                row_ends(1)
                sums(0, 4, 8)
                col_carries(1)
                sums(0, 8, 12)
                col_weights(1)
                sums(0, 12, 16)
                sums(1, 0, 16)

            with pe.Fori(0, LAYERS) as layer:
                pe.wait_ge(s_w_in, layer * 80 + 80)
                hold_waits(pe, s_past[1])
                with pe.Fori(0, GI) as i:
                    g5 = pe.snap((layer * GI + i) * GU)

                    def turn_x(u):
                        pe.wait_ge(s_xs, g5 + (u + 1))
                        hold_waits(pe, s_past[1])
                        for k in range(GB):
                            last = nc.tensor.transpose(ps[0:D, u % 4, k * PART:(k + 1) * PART],
                                                       stage_x[:, u, k, :], ident[:, :])
                        last.then_inc(s_xt, 1)

                    def make_pq(u):
                        pe.wait_ge(s_xtc, g5 + (u + 1))
                        pe.wait_ge(s_qc, g5 + max(u - 3, 0))
                        for k in range(GB):
                            o = ps[:, 4 + u % 4, k * 2 * D:(k + 1) * 2 * D]
                            nc.tensor.matmul(o, ones[:, :], b_ij_sb[:, :], start=True, stop=False)
                            last = nc.tensor.matmul(o, x_t[:, u, k * PART:(k + 1) * PART], w_ij_sb[:, :],
                                                    start=False, stop=True)
                        last.then_inc(s_pq, 1)
                    for u in range(4):
                        turn_x(u)
                    make_pq(0)
                    turn_x(4)
                    for u in range(1, GU):
                        make_pq(u)

                pe.wait_ge(s_p3, layer * (GI * GU) + GI * GU)
                hold_waits(pe, s_past[1])
                with pe.Fori(0, ITERS) as i:
                    g = pe.snap(layer * ITERS + i)
                    g64 = pe.snap(g * 64)
                    g32 = pe.snap(g * 32)
                    g16 = pe.snap(g * 16)
                    g8 = pe.snap(g * 8)
                    g4 = pe.snap(g * 4)

                    def sums(q, lo, hi):
                        if lo == 0:
                            pe.wait_ge(s_relu, g4 + (q + 1))
                        for t in range(lo, hi):
                            tau = H * q + t
                            wait_slot(pe, [s for sb_ in s_acc for s in sb_], g8, tau, H)
                            for j in range(2):
                                last = nc.tensor.matmul(agg_slot(tau)[:, j, 0:D], hot[:, tau, j * PART:(j + 1) * PART],
                                                        rows[:, tau // K, tau % K, :], start=True, stop=True)
                            last.then_inc(s_aggm, 1)

                    for q in range(4):
                        b, h = q // 2, q % 2
                        at = load_blocks(pe, regs, block_row, (i * 4 + q) * H, H)
                        for k in range(4):
                            p = 4 * q + k
                            pe.wait_ge(s_hot, g32 + (2 * p + 2))
                            if p >= 2:
                                pe.wait_ge(s_tc, g16 + (p - 1))
                            for tt in range(2):
                                for j in range(2):
                                    last = nc.tensor.transpose(
                                        t_bank(p)[:, tt * 256 + j * PART:tt * 256 + (j + 1) * PART],
                                        hot[:, 2 * p + tt, j * PART:(j + 1) * PART], ident[:, :])
                            last.then_inc(s_t, 1)
                            if q:
                                sums(q - 1, 2 * k, 2 * k + 2)
                            if k == 0 and h == 0:
                                pe.wait_ge(s_edge[b], g64 + 64)
                            if k == 0 and q >= 2:
                                pe.wait_ge(s_add, g4 + (q - 1))
                            pe.wait_ge(s_tc, g16 + (p + 1))
                            for tt in range(2):
                                t = 2 * k + tt
                                c = h * H + t
                                o = pre_bank(q)[:, t, :]
                                quad = 32 * (c // 4)
                                nc.tensor.matmul(o, edge_f[quad:quad + DE, b, c % 4, :], w_e_sb[quad:quad + DE, :],
                                                 start=True, stop=False)
                                for j in range(2):
                                    for s in range(3):
                                        last = nc.tensor.matmul(
                                            o, hot_t[:, p % 2, tt, j * PART:(j + 1) * PART],
                                            p3[:, ds(at[t] * PW + (j * PW + s * D), D)],
                                            start=False, stop=(j == 1 and s == 2))
                            last.then_inc(s_pre, 1)
                    sums(3, 0, H)

                with pe.Fori(0, GI) as i:
                    g5 = pe.snap((layer * GI + i) * GU)

                    def turn_u(u):
                        pe.wait_ge(s_us, g5 + (u + 1))
                        for k in range(GB):
                            last = nc.tensor.transpose(ps[:, u % 4, k * PART:(k + 1) * PART],
                                                       stage_u[:, u, k, :], ident[:, :])
                        last.then_inc(s_ut, 1)

                    def update(u):
                        pe.wait_ge(s_utc, g5 + (u + 1))
                        pe.wait_ge(s_ux, g5 + max(u - 3, 0))
                        for k in range(GB):
                            o = ps[:, 4 + u % 4, k * D:(k + 1) * D]
                            nc.tensor.matmul(o, ones[:, :], b_u_sb[:, :], start=True, stop=False)
                            last = nc.tensor.matmul(o, stage_ut[:, u, k, :], w_u_sb[:, :],
                                                    start=False, stop=True)
                        last.then_inc(s_up, 1)
                    for u in range(4):
                        turn_u(u)
                    update(0)
                    turn_u(4)
                    for u in range(1, GU):
                        update(u)

        @block.vector
        def _(dve):
            v = nc.vector
            regs = [dve.alloc_register(f"tile_block{k}") for k in range(K)]
            pro = Chain(dve, s_pro)
            dve.wait_ge(s_iota, 1)
            dve.wait_ge(s_in, 16 * N_IN)
            v.memset(ones[:, :], 1.0)
            v.memset(zeros[:, :, :], 0.0)
            v.memset(eps[:, :], EPS)
            v.memset(fwd_chain[:, :, :], -BIG)
            v.memset(bwd_chain[:, :], -BIG)
            v.memset(cat[:, :, :], 0.0)
            v.memset(xn[:, NB:NBP, :], 0.0)
            v.memset(er[:, NB:NBP], 0.0)
            v.tensor_copy(pidx[:, :], pidx_i[:, :])
            pro.link(v.tensor_copy(iota[:, :], iota_i[:, :]))
            pro.link(v.tensor_scalar(ident[:, :], iota[:, 0:PART], pidx[:, :], None, ALU.is_equal))
            pro.link(v.tensor_scalar(resc_col[:, :], pidx[:, :], float(NREST), None, ALU.is_lt))
            pro.link(v.tensor_scalar(xn[:, NT, :], xn[:, NT, :], resc_col[:, :], None, ALU.mult))
            pro.link(v.tensor_scalar(block_row[:, :], first_i, 7, None, ALU.arith_shift_right))
            pro.link(v.tensor_scalar(first_b_i, first_b_i, 7, 7, ALU.arith_shift_right, ALU.logical_shift_left))
            pro.link(v.tensor_tensor(rel[:, :], dst_c_i, first_b_i, ALU.subtract))
            one, cont, chain_f, chain_b = (flags[:, k, :] for k in range(4))
            v.memset(cont[:, 0:1], 0.0)
            v.memset(cont[:, TILES:TILES + 1], 0.0)
            pro.link(v.tensor_tensor(one[:, 0:TILES], first_i, last_i, ALU.is_equal))
            pro.link(v.tensor_tensor(cont[:, 1:TILES], first_i[:, 1:TILES], last_i[:, 0:TILES - 1], ALU.is_equal))
            v.tensor_tensor(chain_f[:, 0:TILES], one[:, 0:TILES], cont[:, 0:TILES], ALU.mult)
            pro.link(v.tensor_tensor(chain_b[:, 0:TILES], one[:, 0:TILES], cont[:, 1:TILES + 1], ALU.mult))
            for f in (cont[:, 0:TILES + 1], chain_f[:, 0:TILES], chain_b[:, 0:TILES]):
                pro.link(v.tensor_scalar(f, f, 2 * BIG, -BIG, ALU.mult, ALU.add))
            prod = big_y
            pro.link(v.tensor_tensor(prod, xn[:, 0:NB, :], ar[:, :].unsqueeze(1).to_broadcast([PART, NB, D]), ALU.mult))
            pro.link(v.tensor_reduce(er[:, 0:NB], prod, AX.X, ALU.add))
            pro.link(v.tensor_copy(er3[:, :, 0], er[:, :]))
            pro.link(v.tensor_tensor(er_rest[:, :], er[:, :], er3[:, :, 0], ALU.subtract))
            pro.link(v.tensor_copy(er3[:, :, 1], er_rest[:, :]))
            pro.link(v.tensor_tensor(er3[:, :, 2], er_rest[:, :], er3[:, :, 1], ALU.subtract))
            v.tensor_copy(resc[:, :], resc_col[0:1, :].to_broadcast([1, 2])).then_inc(s_const, 1)

            with dve.Fori(0, ITERS) as i:
                i128 = dve.snap(i * 128)
                i32 = dve.snap(i * 32)
                i16 = dve.snap(i * 16)
                i2 = dve.snap(i * 2)
                ch = Chain(dve, s_ch0, dve.snap(i * CH0))

                def take_rel(b):
                    ch.link(v.tensor_copy(relc[:, b, :], rel[:, ds((i * 2 + b) * K, K)]))

                def one_hots(b, lo, hi):
                    for t in range(lo, hi):
                        v.tensor_scalar(hot[:, K * b + t, :], iota[:, :], relc[:, b, t:t + 1], None, ALU.is_equal
                                        ).then_inc(s_hot0, 1)

                def scores_src(b):
                    for h in range(2):
                        dve.wait_ge(s_rows0[b][h], i128 + 128)
                    ch.link(v.tensor_tensor(el_prod[:, :, :], rows[:, b, :, :],
                                            al[:, :].unsqueeze(1).to_broadcast([PART, K, D]), ALU.mult))
                    ch.link(v.tensor_reduce(el[:, :], el_prod[:, :, :], AX.X, ALU.add))

                def scores(b):
                    dve.wait_ge(s_er, i16 + (8 * b + 8))
                    ch.link(v.tensor_reduce(ere[:, :], er_bank(b), AX.X, ALU.add))
                    ch.link(v.tensor_tensor(ere[:, :], ere[:, :], el[:, :], ALU.add))
                    v.scalar_tensor_tensor(ec[:, :], ere[:, :], SLOPE, ere[:, :], ALU.mult, ALU.max
                                           ).then_inc(s_ec, 1)
                    dve.wait_ge(s_dstrow[b], i16 + 16)
                    ch.link(v.tensor_tensor(same[:, :], dst_row[:, b, 1:PART + 2], dst_row[:, b, 0:PART + 1], ALU.is_equal))
                    ch.link(v.tensor_scalar(same[:, :], same[:, :], 2 * BIG, -BIG, ALU.mult, ALU.add))

                def scan_rows(b):
                    dve.wait_ge(s_et, i2 + (b + 1))
                    ch.link(v.tensor_copy(e_row[:, :], misc(b)["e_t"]))
                    v.tensor_tensor_scan(fwd[:, :], same[:, 0:PART], e_row[:, :], -BIG, ALU.min, ALU.max)
                    v.tensor_tensor_scan(bwd[:, ::-1], same[:, 1:PART + 1][:, ::-1], e_row[:, ::-1], -BIG,
                                         ALU.min, ALU.max).then_inc(s_ends, 1)

                def chain_rows(b):
                    at = (i * 2 + b) * K
                    dve.wait_ge(s_endst, i2 + (b + 1))
                    ch.link(v.tensor_copy(ends_row[:, :], misc(b)["ends"]))
                    v.tensor_copy(fwd_chain[:, b, 0:1], fwd_chain[:, 1 - b, K:K + 1])
                    v.tensor_tensor_scan(fwd_chain[:, b, 1:K + 1], chain_f[:, ds(at, K)], ends_row[:, 0:K],
                                         fwd_chain[:, 1 - b, K:K + 1], ALU.min, ALU.max)
                    ch.link(v.tensor_copy(carry_row[:, 0:K], chain_b[:, ds(at, K)]))
                    ch.link(v.tensor_tensor_scan(bwd_chain[:, 0:K][:, ::-1], carry_row[:, 0:K][:, ::-1],
                                                 ends_row[:, K:2 * K][:, ::-1], -BIG, ALU.min, ALU.max))
                    v.tensor_tensor(carry_row[:, 0:K], cont[:, ds(at, K)], fwd_chain[:, b, 0:K], ALU.min)
                    v.tensor_tensor(carry_row[:, K:2 * K], cont[:, ds(at + 1, K)], bwd_chain[:, 1:K + 1], ALU.min
                                    ).then_inc(s_carry, 1)

                def maxima(b):
                    dve.wait_ge(s_carryt, i2 + (b + 1))
                    ch.link(v.tensor_copy(carry_col[:, :], misc(b)["carry"]))
                    ch.link(v.tensor_tensor_scan(fwd[:, :], same[:, 0:PART], e_row[:, :], carry_col[:, 0:1],
                                                 ALU.min, ALU.max))
                    ch.link(v.tensor_tensor_scan(bwd[:, ::-1], same[:, 1:PART + 1][:, ::-1], e_row[:, ::-1],
                                                 carry_col[:, 1:2], ALU.min, ALU.max))
                    ch.link(v.tensor_tensor(bwd[:, :], fwd[:, :], bwd[:, :], ALU.max))
                    v.tensor_tensor(shift[:, :], e_row[:, :], bwd[:, :], ALU.subtract).then_inc(s_shift, 1)
                    ch.link(v.tensor_tensor(resc[:, 0:1], fwd_chain[:, b, 0:1], bwd[0:1, 0:1], ALU.subtract))
                    ch.link(v.tensor_scalar(resc[:, 1:2], same[0:1, 0:1], 0.0, 1.0 / BIG, ALU.max, ALU.mult))
                    v.tensor_tensor(resc[:, 0:1], resc[:, 0:1], resc[:, 1:2], ALU.mult).then_inc(s_diff, 1)
                    dve.wait_ge(s_resc, i2 + (b + 1))
                    v.tensor_scalar(resc[:, 0:1], resc[:, 1:2], -1.0, None, ALU.add).then_inc(s_rescm, 1)

                def weigh(b, at0):
                    dve.wait_ge(s_wt, i2 + (b + 1))
                    ch.link(v.tensor_copy(w_col[:, :], misc(b)["w_t"]))
                    v.tensor_copy(weighted[:, b, :, 0], w_col[:, :])
                    v.tensor_tensor(weighted[:, b, :, 1:D + 1], rows[:, b, :, :],
                                    w_col[:, :].unsqueeze(2).to_broadcast([PART, K, D]), ALU.mult
                                    ).then_inc(s_weighted, 1)
                    dve.wait_ge(s_fh, i2 + (b + 1))
                    ch.link(v.tensor_tensor(resc_col[:, :], first_hot[:, b:b + 1], misc(b)["resc"], ALU.mult))
                    ch.link(v.tensor_scalar(resc_col[:, :], resc_col[:, :], 1.0, None, ALU.add))
                    c = cat[:, ds(at0, 1), DEN:CW]
                    ch.link(v.tensor_scalar(c, c, resc_col[:, :], None, ALU.mult))

                def accumulate(b, at, lo, hi):
                    for t in range(lo, hi):
                        dve.wait_ge(s_aggm0, i32 + (K * b + (t | 1) + 1))
                        if t:
                            dve.wait_ge(s_acc0[b], i16 + t)
                        elif b:
                            dve.wait_ge(s_acc0[0], i16 + K)
                        c = cat[:, ds(at[t], 2), DEN:CW]
                        v.tensor_tensor(c, c, agg_slot(K * b + t)[:, :, 0:D + 1], ALU.add).then_inc(s_acc0[b], 1)

                take_rel(0)
                take_rel(1)
                at0 = load_blocks(dve, regs, block_row, i * (2 * K), K)
                one_hots(0, 0, K)
                scores_src(0)
                one_hots(1, 0, 2)
                scores(0)
                one_hots(1, 2, 4)
                scan_rows(0)
                one_hots(1, 4, 8)
                chain_rows(0)
                one_hots(1, 8, 16)
                maxima(0)
                weigh(0, at0[0])
                scores_src(1)
                scores(1)
                accumulate(0, at0, 0, 4)
                scan_rows(1)
                accumulate(0, at0, 4, 8)
                chain_rows(1)
                accumulate(0, at0, 8, 12)
                maxima(1)
                accumulate(0, at0, 12, 16)
                at1 = load_blocks(dve, regs, block_row, i * (2 * K) + K, K)
                weigh(1, at1[0])
                accumulate(1, at1, 0, 16)
                dve.wait_ge(s_acc0[1], i16 + K)
                assert ch.n == CH0, ch.n

            ln = Chain(dve, s_ln)

            def bc(a):
                return a.unsqueeze(2).to_broadcast([PART, NB, D])

            def layernorm(y, z, done_act):
                ln.link(v.tensor_reduce(stat[:, 0, :], y, AX.X, ALU.add))
                ln.link(v.tensor_scalar(stat[:, 0, :], stat[:, 0, :], 1.0 / D, None, ALU.mult))
                ln.link(v.tensor_tensor(y, y, bc(stat[:, 0, :]), ALU.subtract))
                ln.link(v.tensor_tensor(z, y, y, ALU.mult))
                ln.link(v.tensor_reduce(stat[:, 1, :], z, AX.X, ALU.add))
                dve.wait_ge(s_lna, done_act)
                ln.link(v.reciprocal(stat[:, 3, :], stat[:, 2, :]))
                ln.link(v.tensor_tensor(xn[:, 0:NB, :], y, bc(stat[:, 3, :]), ALU.mult))

            r = cat[:, 0:NB, D:CW]
            ln.link(v.tensor_scalar(stat[:, 0, :], cat[:, 0:NB, DEN], 1e-30, None, ALU.max))
            ln.link(v.reciprocal(stat[:, 1, :], stat[:, 0, :]))
            ln.link(v.tensor_tensor(big_y, r, bc(stat[:, 1, :]), ALU.mult))
            ln.link(v.tensor_scalar(big_z, big_y, 0.0, None, ALU.min))
            dve.wait_ge(s_lna, 1)
            ln.link(v.scalar_tensor_tensor(big_y, big_y, 0.0, big_z, ALU.max, ALU.add))
            ln.link(v.scalar_tensor_tensor(big_y, big_y, -1.0, xn[:, 0:NB, :], ALU.add, ALU.add))
            layernorm(big_y, big_z, 2)
            v.memset(cat[:, 0:NB, D:CW], 0.0)
            v.tensor_copy(cat[:, 0:NB, 0:D], xn[:, 0:NB, :]).then_inc(s_x1, 1)
            dve.wait_ge(s_x1, 1)

            with dve.Fori(0, LAYERS) as layer:
                with dve.Fori(0, GI) as i:
                    g = dve.snap(layer * GI + i)
                    g5 = dve.snap(g * GU)
                    g15 = dve.snap(g * (3 * GU))
                    for u in range(GU):
                        if u == 0:
                            dve.wait_ge(s_ux, layer * (GI * GU))
                        v.tensor_copy(stage_x[:, u, :, :], cat[:, ds((i * GU + u) * GB, GB), 0:D]).then_inc(s_xs, 1)
                    for u in range(GU):
                        dve.wait_ge(s_qc, g5 + (u + 1))
                        p_f = stage_pq[:, u, :, 0:D]
                        at = (i * GU + u) * GB
                        part = [p3[:, ds(at * PW, GB * PW)].rearrange("p (b w) -> p b w", w=PW)[:, :, s * D:(s + 1) * D]
                                for s in range(3)]
                        v.tensor_copy(part[0], p_f).then_inc(s_split, 1)
                        dve.wait_ge(s_split, g15 + (3 * u + 1))
                        v.tensor_tensor(p_rest[:, :, :], p_f, part[0], ALU.subtract).then_inc(s_split, 1)
                        dve.wait_ge(s_split, g15 + (3 * u + 2))
                        v.tensor_copy(part[1], p_rest[:, :, :]).then_inc(s_split, 1)
                        dve.wait_ge(s_split, g15 + (3 * u + 3))
                        v.tensor_tensor(part[2], p_rest[:, :, :], part[1], ALU.subtract).then_inc(s_p3, 1)

                for u in range(GU):
                    dve.wait_ge(s_qt[u], layer * (16 * GI) + 16 * GI)
                hold_waits(dve, s_past[2])
                with dve.Fori(0, ITERS) as i:
                    g = dve.snap(layer * ITERS + i)
                    g128 = dve.snap(g * 128)
                    g32 = dve.snap(g * 32)
                    g16 = dve.snap(g * 16)
                    g8 = dve.snap(g * 8)
                    g2 = dve.snap(g * 2)
                    acc = [s for sb_ in s_acc for s in sb_]

                    def one_hots(q, lo, hi):
                        b, h = q // 2, q % 2
                        for t in range(lo, hi):
                            c = h * H + t
                            v.tensor_scalar(hot[:, K * b + c, :], iota[:, :], relc[:, b, c:c + 1], None,
                                            ALU.is_equal).then_inc(s_hot, 1)

                    def accumulate(q, at, lo, hi):
                        for t in range(lo, hi):
                            dve.wait_ge(s_aggm, g32 + (H * q + (t | 1) + 1))
                            if t:
                                dve.wait_ge(acc[q], g8 + t)
                            elif q:
                                dve.wait_ge(acc[q - 1], g8 + H)
                            c = cat[:, ds(at[t], 2), D:CW]
                            v.tensor_tensor(c, c, agg_slot(H * q + t)[:, :, 0:D], ALU.add).then_inc(acc[q], 1)

                    for b in range(2):
                        v.tensor_copy(relc[:, b, :], rel[:, ds((i * 2 + b) * K, K)]).then_inc(s_relc, 1)
                    dve.wait_ge(s_relc, g2 + 2)
                    one_hots(0, 0, H)
                    at = None
                    for q in range(4):
                        b, h = q // 2, q % 2
                        for k in range(4):
                            if q < 3:
                                one_hots(q + 1, 2 * k, 2 * k + 2)
                            if q:
                                accumulate(q - 1, at, 2 * k, 2 * k + 2)
                        dve.wait_ge(s_pre, g16 + 4 * (q + 1))
                        dve.wait_ge(s_rows[b][h], g128 + 128)
                        m = rows[:, b, h * H:h * H + H, :]
                        v.tensor_tensor(m, m, pre_bank(q), ALU.add).then_inc(s_add, 1)
                        at = load_blocks(dve, regs, block_row, (i * 4 + q) * H, H)
                    accumulate(3, at, 0, H)
                    dve.wait_ge(acc[3], g8 + H)

                with dve.Fori(0, GI) as i:
                    g5 = dve.snap((layer * GI + i) * GU)
                    for u in range(GU):
                        v.tensor_copy(stage_u[:, u, :, :], cat[:, ds((i * GU + u) * GB, GB), :]).then_inc(s_us, 1)
                    dve.wait_ge(s_us, g5 + GU)
                    for u in range(GU):
                        v.tensor_copy(cat[:, ds((i * GU + u) * GB, GB), D:CW], zeros[:, :, :]).then_inc(s_uz, 1)
                    dve.wait_ge(s_ux, g5 + GU)
                    dve.wait_ge(s_uz, g5 + GU)

            ln.link(v.tensor_tensor(big_y, cat[:, 0:NB, 0:D], xn[:, 0:NB, :], ALU.add))
            layernorm(big_y, big_z, 3)
            v.engine_nop().then_inc(s_x1, 1)


def dst_rows(dst_flat, at):
    row = dst_flat[0:1, bass.ds(at, K * PART + 2)]
    return bass.AP(tensor=row.tensor, offset=row.offset, ap=[[PART, K], [1, PART + 2]])


def hold_waits(engine, past):
    engine.sem_inc(past, 1)


def load_blocks(engine, regs, block_row, at, n):
    engine.load(regs[:n], block_row[0:1, bass.ds(at, n)])
    return [engine.snap(r, min_val=0, max_val=NB - 1) for r in regs[:n]]


def wait_slot(pe, acc, base, tau, per):
    if tau % 2:
        return
    if tau < 4:
        pe.wait_ge(acc[-1], base)
    else:
        pe.wait_ge(acc[(tau - 3) // per], base + ((tau - 3) % per + 1))


_OUT = ((N, D), "float32")


def kernel(x, src, dst, edge_attr_16, L0_gnn_attn_l, L0_gnn_attn_r, L1_gnn_msg_w, L1_gnn_msg_b,
           L1_gnn_upd_w, L1_gnn_upd_b):
    import concourse.bacc as bacc
    from concourse.bass_utils import run_bass_kernel_spmd

    src, dst, ef = np.asarray(src), np.asarray(dst), np.asarray(edge_attr_16)
    pad = TILES * PART - E
    src_p = np.concatenate([src, np.zeros(pad, src.dtype)])
    dst_p = np.concatenate([dst, np.full(pad, NB * PART - 1, dst.dtype)])
    tiles = dst_p.reshape(TILES, PART)
    mw, uw = np.asarray(L1_gnn_msg_w), np.asarray(L1_gnn_upd_w)
    mb, ub = np.asarray(L1_gnn_msg_b), np.asarray(L1_gnn_upd_b)
    w_e = np.zeros((LAYERS, 4, 32, D), mw.dtype)
    w_e[:, :, 0:DE, :] = mw[:, None, 2 * D:, :]
    arrays = {
        "x": np.asarray(x),
        "src_cols": src_p.reshape(TILES, PART).T,
        "dst_cols": tiles.T,
        "dst_flat": np.concatenate([np.full(1, -1, dst.dtype), dst_p, np.full(1, -1, dst.dtype)])[None],
        "dst_first": tiles[:, 0][None],
        "dst_last": tiles[:, -1][None],
        "edge_t": np.concatenate([ef, np.zeros((pad, DE), ef.dtype)]).T,
        "attn_l": np.asarray(L0_gnn_attn_l)[None],
        "attn_r": np.asarray(L0_gnn_attn_r)[None],
        "w_ij": np.concatenate([mw[:, 0:D], mw[:, D:2 * D]], axis=2).reshape(LAYERS * D, 2 * D),
        "w_e": w_e.reshape(LAYERS * PART, D),
        "w_u": uw.reshape(LAYERS * CW, D),
        "b_ij": np.concatenate([mb, np.zeros_like(mb)], axis=1),
        "b_u": ub,
    }
    arrays = {k: np.ascontiguousarray(a) for k, a in arrays.items()}
    nc = bacc.Bacc("TRN2", target_bir_lowering=False, num_devices=1)
    args = {k: nc.dram_tensor(f"in_{k}", a.shape, mybir.dt.from_np(a.dtype), kind="ExternalInput").ap()
            for k, a in arrays.items()}
    out = nc.dram_tensor("out_0", _OUT[0], F32, kind="ExternalOutput").ap()
    build(nc, out=out, **args)
    result = run_bass_kernel_spmd(nc, [{f"in_{k}": a for k, a in arrays.items()}], core_ids=[0])
    return result.results[0]["out_0"]
```

```python
from contextlib import ExitStack

import numpy as np

import concourse.bass as bass
from concourse import mybir
from concourse.bass import IndirectOffsetOnAxis

F32 = mybir.dt.float32
BF16 = mybir.dt.bfloat16
I32 = mybir.dt.int32
ALU = mybir.AluOpType
ACT = mybir.ActivationFunctionType
AX = mybir.AxisListType

N, D = 12500, 64
E, DE = 212500, 16
LAYERS = 3
PART = 128
K = 16
H = K // 2
TILES = -(-E // (2 * K * PART)) * 2 * K
ITERS = TILES // (2 * K)
NB = -(-N // PART)
GB = 4
GU = 5
GI = -(-NB // (GB * GU))
NBP = GI * GU * GB
NT = NB - 1
NREST = N - NT * PART
BIG = 2.0 ** 126
EPS = 1e-5
SLOPE = 0.2
PW = 3 * D
KE = 7 * DE + 3
N_WE = 7


class Chain:

    def __init__(self, engine, sem, base=0):
        self.engine, self.sem, self.base, self.n = engine, sem, base, 0

    def link(self, ins):
        self.n += 1
        ins.then_inc(self.sem, 1)
        self.engine.wait_ge(self.sem, self.base + self.n)


def held(engine, value):
    return value if isinstance(value, int) else engine.snap(value)


def build(nc, x, src_cols, dst_cols, dst_flat, dst_first, dst_last, edge_t, attn_l, attn_r,
          w_ij, w_e, w_u, b_u, masks, out):
    ds = bass.ds
    ctx = ExitStack()
    with ctx:
        def sb(name, shape, dt=F32):
            return ctx.enter_context(nc.sbuf_tensor(name, shape, dt))

        def sem(name):
            return ctx.enter_context(nc.semaphore(name))

        q_table = nc.dram_tensor("q_table", (NBP * PART, D), F32).ap()
        x1_dram = nc.dram_tensor("x1_dram", (PART, NB * D), F32).ap()
        e_parts = nc.dram_tensor("e_parts", (3 * DE, TILES * PART), BF16).ap()

        xs_t = sb("xs_t", [PART, NBP * PART])
        p3_raw = sb("p3_raw", [PART, max(NBP * PW // 2, 6 * TILES)])
        p3 = p3_raw[:, :].bitcast(BF16)
        agg_raw = sb("agg_raw", [PART, NBP * (D + 1)])
        rows = sb("rows", [PART, 2, K, D])
        n_hot = 2 * K * 2 * PART // 2
        n_win = 2 * H * 2 * PW // 2
        n_msg = 2 * 3 * H * D // 2
        shared = sb("shared", [PART, max(n_hot + n_win + n_msg, NB * D)])
        weighted = sb("weighted", [PART, K, D + 1])
        rel = sb("rel", [PART, TILES + K], BF16)
        relc = sb("relc", [PART, 2, K])
        idx = sb("idx", [PART, 2, K], I32)
        edge_f = sb("edge_f", [PART, 2, K, PART], BF16)
        block_row = sb("block_row", [1, TILES + K], I32)
        hot_t = sb("hot_t", [PART, 2, 2, 2 * PART], BF16)
        iota_i = sb("iota_i", [PART, 2 * PART], I32)
        iota = sb("iota", [PART, 2 * PART], BF16)
        pidx_i = sb("pidx_i", [PART, 1], I32)
        pidx = sb("pidx", [PART, 1])
        ident = sb("ident", [PART, PART])
        ident_b = sb("ident_b", [PART, PART], BF16)
        ones = sb("ones", [1, PART])
        zeros = sb("zeros", [PART, GB, D])
        eps = sb("eps", [PART, 1])
        al = sb("al", [PART, D])
        ar = sb("ar", [PART, D])
        er = sb("er", [PART, NBP])
        er_rest = sb("er_rest", [PART, NBP])
        er3 = sb("er3", [PART, NBP, 3], BF16)
        x_t_raw = sb("x_t_raw", [PART, GU * GB * PART])
        w_ij_sb = sb("w_ij_sb", [D, 2 * D])
        w_e_sb = sb("w_e_sb", [PART, D])
        w_e_rest = sb("w_e_rest", [PART, D])
        w_e_part = sb("w_e_part", [PART, 3, D], BF16)
        w_e7 = sb("w_e7", [PART, D], BF16)
        w_u_sb = sb("w_u_sb", [PART, D])
        b_u_sb = sb("b_u_sb", [D, 1])
        mask = sb("mask", [PART, 3])
        p_rest = sb("p_rest", [PART, GB, D])
        el = sb("el", [PART, K])
        ere = sb("ere", [PART, K])
        ec = sb("ec", [PART, K])
        e_row = sb("e_row", [K, PART])
        dst_row = sb("dst_row", [K, 2, PART + 2], I32)
        same = sb("same", [K, PART + 1])
        fwd = sb("fwd", [K, PART])
        bwd = sb("bwd", [K, PART])
        ends_row = sb("ends_row", [1, 2 * K])
        fwd_chain = sb("fwd_chain", [1, 2, K + 1])
        bwd_chain = sb("bwd_chain", [1, K + 1])
        carry_row = sb("carry_row", [1, 2 * K])
        carry_col = sb("carry_col", [K, 2])
        shift = sb("shift", [K, PART])
        w_row = sb("w_row", [K, PART])
        w_col = sb("w_col", [PART, K])
        resc = sb("resc", [1, 2])
        first_hot = sb("first_hot", [PART, 2])
        resc_col = sb("resc_col", [PART, 1])
        stat = sb("stat", [PART, 4, NB])

        hot = shared[:, 0:n_hot].bitcast(BF16).rearrange("p (t n) -> p t n", n=2 * PART)
        win = shared[:, n_hot:n_hot + n_win].bitcast(BF16).rearrange("p (t w) -> p t w", w=2 * PW)
        msg = shared[:, n_hot + n_win:n_hot + n_win + n_msg].bitcast(BF16).rearrange(
            "p (q s t d) -> p q s t d", q=2, s=3, d=D)
        n_wt = 3 * K * (D + 1) // 2
        wparts = shared[:, n_hot:n_hot + 2 * n_wt].bitcast(BF16).rearrange(
            "p (b s t d) -> p b s t d", b=2, s=3, d=D + 1)
        n_st = GU * GB * D
        stage = shared[:, 0:n_st].rearrange("p (u b d) -> p u b d", u=GU, b=GB)
        stage_pq = shared[:, n_st:3 * n_st].rearrange("p (u b d) -> p u b d", u=GU, b=GB)
        bulk_a = shared[:, 0:NB * D].rearrange("p (b d) -> p b d", d=D)
        bulk_b = p3_raw[:, 0:NB * D].rearrange("p (b d) -> p b d", d=D)
        x_t = x_t_raw[0:D, :].rearrange("p (u n) -> p u n", u=GU)
        agg0 = agg_raw[:, :].rearrange("p (b d) -> p b d", d=D + 1)
        agg = agg_raw[:, 0:NBP * D].rearrange("p (b d) -> p b d", d=D)
        xn = xs_t[:, 0:NBP * D].rearrange("p (b d) -> p b d", d=D)
        FT = TILES + K + 1
        flags = p3[0:1, 0:4 * FT].rearrange("p (f t) -> p f t", f=4)
        el_prod = p3_raw[:, -K * D:].rearrange("p (t d) -> p t d", d=D)
        EW = DE * K
        e_in = x_t_raw[:, 0:2 * EW].rearrange("p (b e) -> p b e", b=2)
        e_out = x_t_raw[:, 2 * EW:5 * EW].bitcast(BF16).rearrange("p (b s e) -> p b s e", b=2, s=3)
        e_rest = x_t_raw[:, 5 * EW:7 * EW].rearrange("p (b e) -> p b e", b=2)
        ints = shared[:, :].bitcast(I32)
        dst_c_i = ints[:, 0:TILES]
        first_b_i = ints[:, TILES:2 * TILES]
        first_i = ints[0:1, 2 * TILES:3 * TILES]
        last_i = ints[0:1, 3 * TILES:4 * TILES]

        ps = ctx.enter_context(nc.psum_tensor("ps", [PART, 8, 512], F32))

        def t_bank(pair):
            return ps[:, pair % 2, 0:256].bitcast(BF16)

        def pre_bank(half):
            return ps[:, 2 + half % 2, :].rearrange("p (t d) -> p t d", d=D)

        def agg_slot(tile):
            return ps[:, 4 + tile % 4 // 2, 256 * (tile % 2):256 * (tile % 2) + 256].rearrange(
                "p (j d) -> p j d", j=2)

        def er_bank(b):
            return ps[:, 2 + b, 0:3 * K].rearrange("p (t s) -> p t s", s=3)

        def misc(b):
            m = ps[:, 6 + b, :]
            return {"e_t": m[0:K, 0:PART], "ends": m[0:1, 128:128 + 2 * K], "carry": m[0:K, 160:162],
                    "w_t": m[:, 192:192 + K], "resc": m[:, 224:225]}

        s_in = sem("s_in")
        s_iota = sem("s_iota")
        s_const = sem("s_const")
        s_pro = sem("s_pro")
        s_past = [sem(f"s_past_{e}") for e in ("pool", "pe", "dve", "act", "sp")]
        s_idx = [sem(f"s_idx{b}") for b in range(2)]
        s_dstrow = [sem(f"s_dstrow{b}") for b in range(2)]
        s_ein = [sem(f"s_ein{b}") for b in range(2)]
        s_eout = [sem(f"s_eout{b}") for b in range(2)]
        s_ehi, s_erest, s_emid, s_elo = (sem(f"s_e_{k}") for k in ("hi", "rest", "mid", "lo"))
        s_rows0 = [sem(f"s_rows0_{b}") for b in range(2)]
        s_hot0 = sem("s_hot0")
        s_t0 = sem("s_t0")
        s_tc0 = sem("s_tc0")
        s_fh = sem("s_fh")
        s_er = sem("s_er")
        s_ec = sem("s_ec")
        s_et = sem("s_et")
        s_ends = sem("s_ends")
        s_endst = sem("s_endst")
        s_carry = sem("s_carry")
        s_carryt = sem("s_carryt")
        s_shift = sem("s_shift")
        s_diff = sem("s_diff")
        s_w = sem("s_w")
        s_resc = sem("s_resc")
        s_rescm = sem("s_rescm")
        s_wt = sem("s_wt")
        s_wf = sem("s_wf")
        s_whi, s_wrest, s_wmid, s_wlo = (sem(f"s_w_{k}") for k in ("hi", "rest", "mid", "lo"))
        s_resd = sem("s_resd")
        s_aggm0 = sem("s_aggm0")
        s_acc0 = sem("s_acc0")
        s_ch0 = sem("s_ch0")
        s_ln = sem("s_ln")
        s_lna = sem("s_lna")
        s_x1 = sem("s_x1")
        s_x1d = sem("s_x1d")
        s_w_in = sem("s_w_in")
        s_we = sem("s_we")
        s_st = sem("s_st")
        s_zero = sem("s_zero")
        s_tr = sem("s_tr")
        s_ca = sem("s_ca")
        s_up = sem("s_up")
        s_rl = sem("s_rl")
        s_keep = sem("s_keep")
        s_pq = sem("s_pq")
        s_qc = sem("s_qc")
        s_split = sem("s_split")
        s_p3 = sem("s_p3")
        s_qt = [sem(f"s_qt{u}") for u in range(GU)]
        s_back = sem("s_back")
        s_fin = sem("s_fin")
        s_rows = [[sem(f"s_rows_{b}{h}") for h in range(2)] for b in range(2)]
        s_edge = [sem(f"s_edge{b}") for b in range(2)]
        s_relc = sem("s_relc")
        s_hot = sem("s_hot")
        s_t = sem("s_t")
        s_tc = sem("s_tc")
        s_pre = sem("s_pre")
        s_add = sem("s_add")
        s_hi, s_rest, s_mid = sem("s_hi"), sem("s_rest"), sem("s_mid")
        s_lo = [sem(f"s_lo{q}") for q in range(4)]
        s_aggm = sem("s_aggm")
        s_acc = sem("s_acc")
        s_out = sem("s_out")
        block = ctx.enter_context(nc.Block())

        N_IN = 10
        CH0 = 42
        PH = GI * GU

        def phases(engine, node, edge):
            node(0)
            with engine.Fori(0, LAYERS - 1) as layer:
                edge(layer)
                node(layer + 1)
            edge(LAYERS - 1)
            node(LAYERS)

        def iterations(engine, n, body):
            body(0, True)
            if n > 1:
                with engine.Fori(1, n) as i:
                    body(i, False)

        @block.sync
        def _(sp):
            sp.dma_start(dst_c_i, dst_cols).then_inc(s_in, 16)
            sp.dma_start(first_b_i, dst_first.partition_broadcast(PART)).then_inc(s_in, 16)
            sp.dma_start(first_i, dst_first).then_inc(s_in, 16)
            sp.dma_start(last_i, dst_last).then_inc(s_in, 16)
            sp.dma_start(al[:, :], attn_l.partition_broadcast(PART)).then_inc(s_in, 16)
            sp.dma_start(ar[:, :], attn_r.partition_broadcast(PART)).then_inc(s_in, 16)
            sp.dma_start(mask[:, :], masks).then_inc(s_in, 16)
            sp.dma_start(xn[:, 0:NT, :], x[0:NT * PART, :].rearrange("(b p) d -> p b d", p=PART)
                         ).then_inc(s_in, 16)
            sp.dma_start(xn[0:NREST, NT, :], x[NT * PART:N, :]).then_inc(s_in, 16)
            sp.dma_start(xn[NREST:PART, NT, :], x[0:PART - NREST, :]).then_inc(s_in, 16)

            e_flat = edge_t.rearrange("f (k e) -> (f k) e", k=PART // DE)
            p_flat = e_parts.rearrange("(s f) (k e) -> (f k) s e", s=3, k=PART // DE)

            def load0(i, first):
                for b in range(2):
                    if not first:
                        sp.wait_ge(s_rows0[b], i * (16 * K))
                    sp.dma_start(idx[:, b, :], src_cols[:, ds((i * 2 + b) * K, K)]).then_inc(s_idx[b], 16)
                    if not first:
                        sp.wait_ge(s_shift, i * 2 + (b - 1))
                    sp.dma_start(dst_row[:, b, :], dst_rows(dst_flat, (i * 2 + b) * (K * PART))
                                 ).then_inc(s_dstrow[b], 16)
                    if not first:
                        sp.wait_ge(s_erest, i * 2 + (b - 1))
                    sp.dma_start(e_in[:, b, :], e_flat[:, ds((i * 2 + b) * EW, EW)]).then_inc(s_ein[b], 16)
                    if first:
                        if b:
                            store_parts(0, 0)
                    else:
                        store_parts(i - (1 - b), 1 - b)

            def store_parts(i, b):
                at = held(sp, (i * 2 + b) * EW)
                sp.wait_ge(s_elo, i * 2 + (b + 1))
                hold_waits(sp, s_past[4])
                sp.dma_start(p_flat[:, :, ds(at, EW)], e_out[:, b, :, :]).then_inc(s_eout[b], 16)

            def load_weights(n):
                sp.dma_start(w_ij_sb[:, :], w_ij[ds(n * D, D), :]).then_inc(s_w_in, 16)
                sp.dma_start(w_e_sb[:, :], w_e[ds(n * PART, PART), :]).then_inc(s_w_in, 16)
                sp.dma_start(w_u_sb[:, :], w_u[ds(n * PART, PART), :]).then_inc(s_w_in, 16)
                sp.dma_start(b_u_sb[:, :], b_u[ds(n * D, D), :]).then_inc(s_w_in, 16)

            load_weights(0)
            iterations(sp, ITERS, load0)
            store_parts(ITERS - 1, 1)

            sp.wait_ge(s_x1, 1)
            sp.dma_start(x1_dram, agg_raw[:, 0:NB * D]).then_inc(s_x1d, 16)
            for b in range(2):
                sp.wait_ge(s_eout[b], 16 * ITERS)

            def node(n):
                if isinstance(n, int) and n == LAYERS:
                    sp.wait_ge(s_acc, LAYERS * TILES)
                    sp.dma_start(p3_raw[:, 0:NB * D], x1_dram).then_inc(s_x1d, 16)
                    return
                rows_q = q_table.rearrange("(b p) d -> p b d", p=PART)

                def store_q(i, first):
                    g5 = held(sp, (n * GI + i) * GU)
                    for u in range(GU):
                        sp.wait_ge(s_qc, g5 + (u + 1))
                        sp.dma_start(rows_q[:, ds((i * GU + u) * GB, GB), :], stage_pq[:, u, :, D:2 * D]
                                     ).then_inc(s_qt[u], 16)
                iterations(sp, GI, store_q)
                sp.wait_ge(s_p3, n * PH + PH)
                load_weights(n + 1)

            def edge(layer):
                def load(i, first):
                    g = held(sp, layer * ITERS + i)
                    for b in range(2):
                        if not first:
                            for h in range(2):
                                sp.wait_ge(s_rows[b][h], g * (16 * H))
                        sp.dma_start(idx[:, b, :], src_cols[:, ds((i * 2 + b) * K, K)]).then_inc(s_idx[b], 16)
                        if not first:
                            sp.wait_ge(s_pre, g * 16 + (8 * b - 8))
                        cols = ds((i * 2 + b) * (K * PART), K * PART)
                        for r in range(3):
                            sp.dma_start(edge_f[32 * r:32 * r + 32, b, :, :].rearrange("p t e -> p (t e)"),
                                         e_parts[0:32, cols]).then_inc(s_edge[b], 16)
                        sp.dma_start(edge_f[96:96 + DE, b, :, :].rearrange("p t e -> p (t e)"),
                                     e_parts[32:32 + DE, cols]).then_inc(s_edge[b], 16)
                iterations(sp, ITERS, load)

            phases(sp, node, edge)

            sp.wait_ge(s_x1, 2)
            res = agg_raw[:, 0:NB * D].rearrange("p (b d) -> p b d", d=D)
            sp.dma_start(out[0:NT * PART, :].rearrange("(b p) d -> p b d", p=PART), res[:, 0:NT, :]
                         ).then_inc(s_out, 16)
            sp.dma_start(out[NT * PART:N, :], res[0:NREST, NT, :]).then_inc(s_out, 16)
            sp.wait_ge(s_out, 32)

        @block.gpsimd
        def _(pool):
            nc.gpsimd.iota(iota_i[:, :], [[1, 2 * PART]], base=0, channel_multiplier=0)
            nc.gpsimd.iota(pidx_i[:, :], [[1, 1]], base=0, channel_multiplier=1).then_inc(s_iota, 1)

            def gather(table, b, lo, hi, s):
                for t in range(lo, hi):
                    nc.gpsimd.indirect_dma_start(
                        rows[:, b, t, :], None, table,
                        IndirectOffsetOnAxis(ap=idx[:, b, t:t + 1], axis=0)).then_inc(s, 16)

            def gather0(i, first):
                for b in range(2):
                    pool.wait_ge(s_idx[b], i * 16 + 16)
                    if not first:
                        pool.wait_ge(s_wf, i * 2 + (b - 1))
                    hold_waits(pool, s_past[0])
                    gather(x, b, 0, K, s_rows0[b])
            iterations(pool, ITERS, gather0)

            def node(n):
                last = isinstance(n, int) and n == LAYERS
                if last:
                    return
                if isinstance(n, int) and n == 0:
                    pool.wait_ge(s_x1d, 16)

                def group(i, first):
                    g5 = held(pool, (n * GI + i) * GU)
                    for u in range(GU):
                        pool.wait_ge(s_st, g5 + (u + 1))
                        hold_waits(pool, s_past[0])
                        nc.gpsimd.tensor_copy(agg[:, ds((i * GU + u) * GB, GB), :], zeros[:, :, :]
                                              ).then_inc(s_zero, 1)
                    for u in range(GU):
                        pool.wait_ge(s_rl, g5 + (u + 1))
                        hold_waits(pool, s_past[0])
                        nc.gpsimd.tensor_copy(xs_t[0:D, ds((i * GU + u) * (GB * PART), GB * PART)], x_t[:, u, :]
                                              ).then_inc(s_keep, 1)
                iterations(pool, GI, group)

            def edge(layer):
                for u in range(GU):
                    pool.wait_ge(s_qt[u], layer * (16 * GI) + 16 * GI)
                hold_waits(pool, s_past[0])

                def gathers(i, first):
                    g = held(pool, layer * ITERS + i)
                    for b in range(2):
                        for h in range(2):
                            if h == 0:
                                pool.wait_ge(s_idx[b], g * 16 + (16 * ITERS + 16))
                            if not first:
                                pool.wait_ge(s_lo[2 * b + h], g)
                            if h == 0 or not first:
                                hold_waits(pool, s_past[0])
                            gather(q_table, b, h * H, h * H + H, s_rows[b][h])
                iterations(pool, ITERS, gathers)

            phases(pool, node, edge)

        @block.scalar
        def _(act):
            act.wait_ge(s_const, 1)

            def copy_pairs(base16, c, lo, hi):
                for k in range(lo, hi):
                    p = 8 * c + k
                    act.wait_ge(s_t0, base16 + (p + 1))
                    if not (isinstance(base16, int) and base16 + p < 2):
                        act.wait_ge(s_er, base16 + (p - 1))
                    if k == 0:
                        nc.scalar.copy(first_hot[:, c % 2:c % 2 + 1], t_bank(p)[:, 0:1]).then_inc(s_fh, 1)
                    nc.scalar.copy(hot_t[:, p % 2, :, :].rearrange("p a b -> p (a b)"), t_bank(p)
                                   ).then_inc(s_tc0, 1)

            def parts0(i2, c):
                act.wait_ge(s_wf, i2 + (c + 1))
                nc.scalar.copy(wparts[:, c % 2, 0, :, :], weighted[:, :, :]).then_inc(s_whi, 1)
                act.wait_ge(s_wrest, i2 + (c + 1))
                nc.scalar.copy(wparts[:, c % 2, 1, :, :], weighted[:, :, :]).then_inc(s_wmid, 1)

            def iter0(i, first):
                i16, i2 = held(act, i * 16), held(act, i * 2)
                for b in range(2):
                    if not (first and b == 0):
                        parts0(i2, b - 1)
                    act.wait_ge(s_ein[b], i * 16 + 16)
                    if not first:
                        act.wait_ge(s_eout[b], i * 16)
                    nc.scalar.copy(e_out[:, b, 0, :], e_in[:, b, :]).then_inc(s_ehi, 1)
                    copy_pairs(i16, b + 1, 0, 4)
                    act.wait_ge(s_erest, i2 + (b + 1))
                    nc.scalar.copy(e_out[:, b, 1, :], e_rest[:, b, :]).then_inc(s_emid, 1)
                    copy_pairs(i16, b + 1, 4, 6)
                    act.wait_ge(s_shift, i2 + (b + 1))
                    nc.scalar.activation(w_row[:, :], shift[:, :], ACT.Exp).then_inc(s_w, 1)
                    act.wait_ge(s_diff, i2 + (b + 1))
                    nc.scalar.activation(resc[:, 1:2], resc[:, 0:1], ACT.Exp).then_inc(s_resc, 1)
                    copy_pairs(i16, b + 1, 6, 8)

            copy_pairs(0, 0, 0, 8)
            iterations(act, ITERS, iter0)
            parts0(2 * ITERS, -1)

            def root(n):
                act.wait_ge(s_ln, n)
                nc.scalar.activation(stat[:, 2, :], stat[:, 1, :], ACT.Sqrt, bias=eps[:, :],
                                     scale=1.0 / D).then_inc(s_lna, 1)

            act.wait_ge(s_ln, 4)
            nc.scalar.activation(bulk_b, bulk_b, ACT.Exp).then_inc(s_lna, 1)
            root(11)

            def node(n):
                fresh = isinstance(n, int) and n == 0
                end = isinstance(n, int) and n == LAYERS

                def group(i, first):
                    g5 = held(act, (n * GI + i) * GU)

                    def turned(u):
                        act.wait_ge(s_tr, g5 + (u + 1))
                        t = ps[0:D, u % 2, :]
                        if fresh:
                            if not first:
                                act.wait_ge(s_keep, g5)
                            nc.scalar.copy(x_t[:, u, :], t).then_inc(s_rl, 1)
                        else:
                            hold_waits(act, s_past[3])
                            nc.scalar.copy(xs_t[D:2 * D, ds((i * GU + u) * (GB * PART), GB * PART)], t
                                           ).then_inc(s_ca, 1)

                    def relu(u):
                        act.wait_ge(s_up, g5 + (u + 1) - PH)
                        if not first and not end:
                            act.wait_ge(s_keep, g5)
                        nc.scalar.activation(x_t[:, u, :], ps[0:D, 2 + u % 2, :], ACT.Relu, bias=b_u_sb[:, :]
                                             ).then_inc(s_rl, 1)

                    def copy_pq(u):
                        act.wait_ge(s_pq, g5 + (u + 1))
                        if not first:
                            act.wait_ge(s_qt[u], (n * GI + i) * 16)
                            act.wait_ge(s_p3, g5)
                        nc.scalar.copy(stage_pq[:, u, :, :].rearrange("p b d -> p (b d)"), ps[:, 4 + u % 4, :]
                                       ).then_inc(s_qc, 1)

                    for u in range(GU + 2):
                        if u < GU:
                            turned(u)
                        if not fresh and 1 <= u < GU + 1:
                            relu(u - 1)
                        if not end and u >= 2:
                            copy_pq(u - 2)
                iterations(act, GI, group)

            def edge(layer):
                def part_hi(g4, q):
                    act.wait_ge(s_add, g4 + (q + 1))
                    nc.scalar.activation(msg[:, q % 2, 0, :, :], rows[:, q // 2 % 2, q % 2 * H:q % 2 * H + H, :],
                                         ACT.Relu).then_inc(s_hi, 1)

                def part_mid(g4, q):
                    act.wait_ge(s_rest, g4 + (q + 1))
                    nc.scalar.copy(msg[:, q % 2, 1, :, :], rows[:, q // 2 % 2, q % 2 * H:q % 2 * H + H, :]
                                   ).then_inc(s_mid, 1)

                def halves(i, first):
                    g = held(act, layer * ITERS + i)
                    g16, g4 = held(act, g * 16), held(act, g * 4)
                    for q in range(4):
                        lag = not (first and q == 0)
                        for k in range(4):
                            if k == 0 and lag:
                                part_hi(g4, q - 1)
                            if k == 1 and lag:
                                part_mid(g4, q - 1)
                            p = 4 * q + k
                            act.wait_ge(s_t, g16 + (p + 1))
                            if not first or p >= 2:
                                act.wait_ge(s_pre, g16 + (p - 1))
                            nc.scalar.copy(hot_t[:, p % 2, :, :].rearrange("p a b -> p (a b)"), t_bank(p)
                                           ).then_inc(s_tc, 1)
                iterations(act, ITERS, halves)
                g4 = held(act, layer * (4 * ITERS) + 4 * ITERS)
                part_hi(g4, -1)
                part_mid(g4, -1)

            phases(act, node, edge)
            root(18)

        @block.tensor
        def _(pe):
            regs = [pe.alloc_register(f"tile_block{k}") for k in range(K)]
            er3_f = er3[:, :, :].rearrange("p b s -> p (b s)")
            pe.wait_ge(s_const, 1)

            def er_pairs(i, i32, i16, i2, c, lo, hi):
                at = load_blocks(pe, regs, block_row, (i * 2 + c) * K + 2 * lo, 2 * (hi - lo))
                for k in range(lo, hi):
                    p = 8 * c + k
                    pe.wait_ge(s_hot0, i32 + (2 * p + 2))
                    for tt in range(2):
                        for j in range(2):
                            last = nc.tensor.transpose(
                                t_bank(p)[:, tt * 256 + j * PART:tt * 256 + (j + 1) * PART],
                                hot[:, (2 * p + tt) % (2 * K), j * PART:(j + 1) * PART], ident_b[:, :])
                    last.then_inc(s_t0, 1)
                    pe.wait_ge(s_tc0, i16 + (p + 1))
                    if k == 0 and not (isinstance(i2, int) and i2 + c < 2):
                        pe.wait_ge(s_ec, i2 + (c - 1))
                    for tt in range(2):
                        for j in range(2):
                            last = nc.tensor.matmul(
                                er_bank(c % 2)[:, 2 * k + tt, :], hot_t[:, p % 2, tt, j * PART:(j + 1) * PART],
                                er3_f[:, ds(at[2 * (k - lo) + tt] * 3 + 3 * j, 3)], start=(j == 0), stop=(j == 1))
                    last.then_inc(s_er, 1)

            def sums0(i32, i2, c, lo, hi, start=False):
                if lo == 0:
                    pe.wait_ge(s_wlo, i2 + (c + 1))
                for t in range(lo, hi):
                    tau = K * c + t
                    if t % 2 == 0 and not (start and t < 4):
                        pe.wait_ge(s_acc0, i32 + (tau - 2))
                    for j in range(2):
                        for s in range(3):
                            last = nc.tensor.matmul(
                                agg_slot(tau)[:, j, 0:D + 1], hot[:, tau % (2 * K), j * PART:(j + 1) * PART],
                                wparts[:, c % 2, s, t, :], start=(s == 0), stop=(s == 2))
                    last.then_inc(s_aggm0, 1)

            def iter0(i, first):
                i32, i16, i2 = held(pe, i * 32), held(pe, i * 16), held(pe, i * 2)
                for b in range(2):
                    prev = not (first and b == 0)
                    start = first and b == 1
                    m = misc(b)
                    pe.wait_ge(s_ec, i2 + (b + 1))
                    nc.tensor.transpose(m["e_t"], ec[:, :], ident[:, :]).then_inc(s_et, 1)
                    if prev:
                        sums0(i32, i2, b - 1, 0, 4, start)
                    er_pairs(i, i32, i16, i2, b + 1, 0, 2)
                    pe.wait_ge(s_ends, i2 + (b + 1))
                    hold_waits(pe, s_past[1])
                    nc.tensor.transpose(m["ends"][:, 0:K], fwd[:, PART - 1:PART], ident[0:K, 0:K])
                    nc.tensor.transpose(m["ends"][:, K:2 * K], bwd[:, 0:1], ident[0:K, 0:K]).then_inc(s_endst, 1)
                    if prev:
                        sums0(i32, i2, b - 1, 4, 8)
                    er_pairs(i, i32, i16, i2, b + 1, 2, 4)
                    pe.wait_ge(s_carry, i2 + (b + 1))
                    hold_waits(pe, s_past[1])
                    nc.tensor.transpose(m["carry"][:, 0:1], carry_row[:, 0:K], ident[0:1, 0:1])
                    nc.tensor.transpose(m["carry"][:, 1:2], carry_row[:, K:2 * K], ident[0:1, 0:1]
                                        ).then_inc(s_carryt, 1)
                    if prev:
                        sums0(i32, i2, b - 1, 8, 12)
                    er_pairs(i, i32, i16, i2, b + 1, 4, 6)
                    if prev:
                        sums0(i32, i2, b - 1, 12, 16)
                    er_pairs(i, i32, i16, i2, b + 1, 6, 8)
                    pe.wait_ge(s_w, i2 + (b + 1))
                    hold_waits(pe, s_past[1])
                    nc.tensor.transpose(m["w_t"], w_row[:, :], ident[0:K, 0:K])
                    pe.wait_ge(s_rescm, i2 + (b + 1))
                    nc.tensor.matmul(m["resc"], ones[:, :], resc[:, 0:1], start=True, stop=True
                                     ).then_inc(s_wt, 1)

            er_pairs(0, 0, 0, 0, 0, 0, 8)
            iterations(pe, ITERS, iter0)
            sums0(32 * ITERS, 2 * ITERS, -1, 0, K)

            def node(n):
                fresh = isinstance(n, int) and n == 0
                end = isinstance(n, int) and n == LAYERS
                pe.wait_ge(s_w_in, n * 64 + 64)
                if not fresh:
                    pe.wait_ge(s_keep, n * PH)

                def group(i, first):
                    g5 = held(pe, (n * GI + i) * GU)

                    def turn(u):
                        pe.wait_ge(s_st, g5 + (u + 1))
                        if fresh and u >= 2:
                            pe.wait_ge(s_rl, g5 + (u - 1))
                        hold_waits(pe, s_past[1])
                        for k in range(GB):
                            last = nc.tensor.transpose(ps[0:D, u % 2, k * PART:(k + 1) * PART],
                                                       stage[:, u, k, :], ident[:, :])
                        last.then_inc(s_tr, 1)

                    def update(u):
                        pe.wait_ge(s_ca, g5 + (u + 1) - PH)
                        if u >= 2:
                            pe.wait_ge(s_rl, g5 + (u - 1))
                        hold_waits(pe, s_past[1])
                        nc.tensor.matmul(ps[0:D, 2 + u % 2, :], w_u_sb[:, :],
                                         xs_t[:, ds((i * GU + u) * (GB * PART), GB * PART)],
                                         start=True, stop=True).then_inc(s_up, 1)

                    def make_pq(u):
                        pe.wait_ge(s_rl, g5 + (u + 1))
                        if u == 4:
                            pe.wait_ge(s_qc, g5 + 1)
                        hold_waits(pe, s_past[1])
                        for k in range(GB):
                            last = nc.tensor.matmul(ps[:, 4 + u % 4, k * 2 * D:(k + 1) * 2 * D],
                                                    x_t[:, u, k * PART:(k + 1) * PART], w_ij_sb[:, :],
                                                    start=True, stop=True)
                        last.then_inc(s_pq, 1)

                    def turn_back(u):
                        pe.wait_ge(s_rl, g5 + (u + 1))
                        if not first or u == 4:
                            pe.wait_ge(s_fin, held(pe, i * GU) + (u - 3))
                        hold_waits(pe, s_past[1])
                        for k in range(GB):
                            last = nc.tensor.transpose(ps[:, 4 + u % 4, k * D:(k + 1) * D],
                                                       x_t[:, u, k * PART:(k + 1) * PART], ident[0:D, 0:D])
                        last.then_inc(s_back, 1)

                    for u in range(GU + 2):
                        if u < GU:
                            turn(u)
                        if not fresh and 1 <= u < GU + 1:
                            update(u - 1)
                        if u >= 2:
                            turn_back(u - 2) if end else make_pq(u - 2)
                iterations(pe, GI, group)

            def edge(layer):
                def sums(g, g32, q, lo, hi, start=False):
                    if lo == 0:
                        pe.wait_ge(s_lo[q % 4], g + (q // 4 + 1))
                    for t in range(lo, hi):
                        tau = H * q + t
                        if t % 2 == 0 and not (start and t < 4):
                            pe.wait_ge(s_acc, g32 + (tau - 2))
                        for j in range(2):
                            for s in range(3):
                                last = nc.tensor.matmul(
                                    agg_slot(tau)[:, j, 0:D], hot[:, tau % (2 * K), j * PART:(j + 1) * PART],
                                    msg[:, q % 2, s, t, :], start=(s == 0), stop=(s == 2))
                        last.then_inc(s_aggm, 1)

                def halves(i, first):
                    g = held(pe, layer * ITERS + i)
                    g32, g16, g4 = held(pe, g * 32), held(pe, g * 16), held(pe, g * 4)
                    hb = held(pe, layer * (TILES + H) + i * 32)
                    for q in range(4):
                        b, h = q // 2, q % 2
                        for k in range(4):
                            p = 4 * q + k
                            pe.wait_ge(s_hot, hb + (2 * p + 2))
                            for tt in range(2):
                                for j in range(2):
                                    last = nc.tensor.transpose(
                                        t_bank(p)[:, tt * 256 + j * PART:tt * 256 + (j + 1) * PART],
                                        hot[:, 2 * p + tt, j * PART:(j + 1) * PART], ident_b[:, :])
                            last.then_inc(s_t, 1)
                            if not first or q >= 2:
                                sums(g, g32, q - 2, 2 * k, 2 * k + 2, start=first and q == 2)
                            if k == 0 and h == 0:
                                pe.wait_ge(s_edge[b], g * 64 + 64)
                            if k == 0 and (not first or q >= 2):
                                pe.wait_ge(s_add, g4 + (q - 1))
                            pe.wait_ge(s_tc, g16 + (p + 1))
                            for tt in range(2):
                                t = 2 * k + tt
                                o = pre_bank(q)[:, t, :]
                                nc.tensor.matmul(o, edge_f[0:KE, b, h * H + t, :], w_e7[0:KE, :],
                                                 start=True, stop=False)
                                for j in range(2):
                                    for s in range(3):
                                        last = nc.tensor.matmul(
                                            o, hot_t[:, p % 2, tt, j * PART:(j + 1) * PART],
                                            win[:, H * (q % 2) + t, j * PW + s * D:j * PW + (s + 1) * D],
                                            start=False, stop=(j == 1 and s == 2))
                            last.then_inc(s_pre, 1)

                pe.wait_ge(s_we, layer * N_WE + N_WE)
                iterations(pe, ITERS, halves)
                g = held(pe, layer * ITERS + ITERS)
                g32 = held(pe, g * 32)
                sums(g, g32, -2, 0, H)
                sums(g, g32, -1, 0, H)

            phases(pe, node, edge)

        @block.vector
        def _(dve):
            v = nc.vector
            regs = [dve.alloc_register(f"tile_block{k}") for k in range(2 * K)]
            pro = Chain(dve, s_pro)
            dve.wait_ge(s_iota, 1)
            dve.wait_ge(s_in, 16 * N_IN)
            v.memset(ones[:, :], 1.0)
            v.memset(zeros[:, :, :], 0.0)
            v.memset(eps[:, :], EPS)
            v.memset(fwd_chain[:, :, :], -BIG)
            v.memset(bwd_chain[:, :], -BIG)
            v.memset(agg_raw[:, :], 0.0)
            v.memset(rel[:, TILES:TILES + K], 0.0)
            v.memset(block_row[:, TILES:TILES + K], 0)
            v.memset(er[:, NB:NBP], 0.0)
            v.tensor_copy(pidx[:, :], pidx_i[:, :])
            pro.link(v.tensor_copy(iota[:, :], iota_i[:, :]))
            v.tensor_scalar(ident[:, :], iota[:, 0:PART], pidx[:, :], None, ALU.is_equal)
            v.tensor_scalar(ident_b[:, :], iota[:, 0:PART], pidx[:, :], None, ALU.is_equal)
            pro.link(v.tensor_scalar(resc_col[:, :], pidx[:, :], float(NREST), None, ALU.is_lt))
            pro.link(v.tensor_scalar(xn[:, NT, :], xn[:, NT, :], resc_col[:, :], None, ALU.mult))
            pro.link(v.tensor_scalar(block_row[:, 0:TILES], first_i, 7, None, ALU.arith_shift_right))
            pro.link(v.tensor_scalar(first_b_i, first_b_i, 7, 7, ALU.arith_shift_right, ALU.logical_shift_left))
            pro.link(v.tensor_tensor(rel[:, 0:TILES], dst_c_i, first_b_i, ALU.subtract))
            one, cont, chain_f, chain_b = (flags[:, k, :] for k in range(4))
            pro.link(v.memset(flags[:, :, :], 0.0))
            v.tensor_tensor(one[:, 0:TILES], first_i, last_i, ALU.is_equal)
            pro.link(v.tensor_tensor(cont[:, 1:TILES], first_i[:, 1:TILES], last_i[:, 0:TILES - 1], ALU.is_equal))
            v.tensor_tensor(chain_f[:, 0:TILES], one[:, 0:TILES], cont[:, 0:TILES], ALU.mult)
            pro.link(v.tensor_tensor(chain_b[:, 0:TILES], one[:, 0:TILES], cont[:, 1:TILES + 1], ALU.mult))
            pro.link(v.tensor_scalar(flags[:, 1:4, :], flags[:, 1:4, :], 2 * BIG, -BIG, ALU.mult, ALU.add))
            pro.link(v.tensor_tensor(bulk_a, xn[:, 0:NB, :], ar[:, :].unsqueeze(1).to_broadcast([PART, NB, D]), ALU.mult))
            pro.link(v.tensor_reduce(er[:, 0:NB], bulk_a, AX.X, ALU.add))
            pro.link(v.tensor_copy(er3[:, :, 0], er[:, :]))
            pro.link(v.tensor_tensor(er_rest[:, :], er[:, :], er3[:, :, 0], ALU.subtract))
            pro.link(v.tensor_copy(er3[:, :, 1], er_rest[:, :]))
            v.tensor_tensor(er3[:, :, 2], er_rest[:, :], er3[:, :, 1], ALU.subtract).then_inc(s_const, 1)

            def one_hots0(b, lo, hi):
                for t in range(lo, hi):
                    v.tensor_scalar(hot[:, K * b + t, :], iota[:, :], relc[:, b, t:t + 1], None, ALU.is_equal
                                    ).then_inc(s_hot0, 1)

            def accumulate0(i32, c, at, lo, hi):
                for t in range(lo, hi):
                    dve.wait_ge(s_aggm0, i32 + (K * c + (t | 1) + 1))
                    if t:
                        dve.wait_ge(s_acc0, i32 + (K * c + t))
                    a = agg0[:, ds(at[t - lo], 2), :]
                    v.tensor_tensor(a, a, agg_slot(K * c + t)[:, :, 0:D + 1], ALU.add).then_inc(s_acc0, 1)

            def part_rest(i2, c):
                dve.wait_ge(s_whi, i2 + (c + 1))
                v.tensor_tensor(weighted[:, :, :], weighted[:, :, :], wparts[:, c % 2, 0, :, :], ALU.subtract
                                ).then_inc(s_wrest, 1)

            def part_lo(i2, c):
                dve.wait_ge(s_wmid, i2 + (c + 1))
                v.tensor_tensor(wparts[:, c % 2, 2, :, :], weighted[:, :, :], wparts[:, c % 2, 1, :, :], ALU.subtract
                                ).then_inc(s_wlo, 1)

            def iter0(i, first):
                i32, i16, i2 = held(dve, i * 32), held(dve, i * 16), held(dve, i * 2)
                ch = Chain(dve, s_ch0, held(dve, i * CH0))
                for b in range(2):
                    prev = not (first and b == 0)

                    ch.link(v.tensor_copy(relc[:, 1 - b, :], rel[:, ds((i * 2 + b + 1) * K, K)]))
                    if prev:
                        part_rest(i2, b - 1)
                    dve.wait_ge(s_rows0[b], i * (16 * K) + 16 * K)
                    ch.link(v.tensor_tensor(el_prod, rows[:, b, :, :],
                                            al[:, :].unsqueeze(1).to_broadcast([PART, K, D]), ALU.mult))
                    ch.link(v.tensor_reduce(el[:, :], el_prod, AX.X, ALU.add))
                    dve.wait_ge(s_er, i16 + (8 * b + 8))
                    ch.link(v.tensor_reduce(ere[:, :], er_bank(b), AX.X, ALU.add))
                    ch.link(v.tensor_tensor(ere[:, :], ere[:, :], el[:, :], ALU.add))
                    v.scalar_tensor_tensor(ec[:, :], ere[:, :], SLOPE, ere[:, :], ALU.mult, ALU.max
                                           ).then_inc(s_ec, 1)
                    if prev:
                        part_lo(i2, b - 1)
                    dve.wait_ge(s_dstrow[b], i16 + 16)
                    ch.link(v.tensor_tensor(same[:, :], dst_row[:, b, 1:PART + 2], dst_row[:, b, 0:PART + 1], ALU.is_equal))
                    ch.link(v.tensor_scalar(same[:, :], same[:, :], 2 * BIG, -BIG, ALU.mult, ALU.add))

                    def fill(k):
                        if prev:
                            at = load_blocks(dve, regs, block_row, (i * 2 + b - 1) * K + 4 * k, 4)
                            accumulate0(i32, b - 1, at, 4 * k, 4 * k + 4)
                        one_hots0(1 - b, 4 * k, 4 * k + 4)

                    dve.wait_ge(s_et, i2 + (b + 1))
                    ch.link(v.tensor_copy(e_row[:, :], misc(b)["e_t"]))
                    v.tensor_tensor_scan(fwd[:, :], same[:, 0:PART], e_row[:, :], -BIG, ALU.min, ALU.max)
                    v.tensor_tensor_scan(bwd[:, ::-1], same[:, 1:PART + 1][:, ::-1], e_row[:, ::-1], -BIG,
                                         ALU.min, ALU.max).then_inc(s_ends, 1)
                    fill(0)
                    at = (i * 2 + b) * K
                    dve.wait_ge(s_endst, i2 + (b + 1))
                    ch.link(v.tensor_copy(ends_row[:, :], misc(b)["ends"]))
                    v.tensor_copy(fwd_chain[:, b, 0:1], fwd_chain[:, 1 - b, K:K + 1])
                    v.tensor_tensor_scan(fwd_chain[:, b, 1:K + 1], chain_f[:, ds(at, K)], ends_row[:, 0:K],
                                         fwd_chain[:, 1 - b, K:K + 1], ALU.min, ALU.max)
                    ch.link(v.tensor_copy(carry_row[:, 0:K], chain_b[:, ds(at, K)]))
                    ch.link(v.tensor_tensor_scan(bwd_chain[:, 0:K][:, ::-1], carry_row[:, 0:K][:, ::-1],
                                                 ends_row[:, K:2 * K][:, ::-1], -BIG, ALU.min, ALU.max))
                    v.tensor_tensor(carry_row[:, 0:K], cont[:, ds(at, K)], fwd_chain[:, b, 0:K], ALU.min)
                    v.tensor_tensor(carry_row[:, K:2 * K], cont[:, ds(at + 1, K)], bwd_chain[:, 1:K + 1], ALU.min
                                    ).then_inc(s_carry, 1)
                    fill(1)
                    dve.wait_ge(s_carryt, i2 + (b + 1))
                    ch.link(v.tensor_copy(carry_col[:, :], misc(b)["carry"]))
                    ch.link(v.tensor_tensor_scan(fwd[:, :], same[:, 0:PART], e_row[:, :], carry_col[:, 0:1],
                                                 ALU.min, ALU.max))
                    ch.link(v.tensor_tensor_scan(bwd[:, ::-1], same[:, 1:PART + 1][:, ::-1], e_row[:, ::-1],
                                                 carry_col[:, 1:2], ALU.min, ALU.max))
                    ch.link(v.tensor_tensor(bwd[:, :], fwd[:, :], bwd[:, :], ALU.max))
                    v.tensor_tensor(shift[:, :], e_row[:, :], bwd[:, :], ALU.subtract).then_inc(s_shift, 1)
                    ch.link(v.tensor_tensor(resc[:, 0:1], fwd_chain[:, b, 0:1], bwd[0:1, 0:1], ALU.subtract))
                    ch.link(v.tensor_scalar(resc[:, 1:2], same[0:1, 0:1], 0.0, 1.0 / BIG, ALU.max, ALU.mult))
                    v.tensor_tensor(resc[:, 0:1], resc[:, 0:1], resc[:, 1:2], ALU.mult).then_inc(s_diff, 1)
                    fill(2)
                    dve.wait_ge(s_ehi, i2 + (b + 1))
                    v.tensor_tensor(e_rest[:, b, :], e_in[:, b, :], e_out[:, b, 0, :], ALU.subtract
                                    ).then_inc(s_erest, 1)
                    dve.wait_ge(s_resc, i2 + (b + 1))
                    v.tensor_scalar(resc[:, 0:1], resc[:, 1:2], -1.0, None, ALU.add).then_inc(s_rescm, 1)
                    fill(3)
                    dve.wait_ge(s_emid, i2 + (b + 1))
                    v.tensor_tensor(e_out[:, b, 2, :], e_rest[:, b, :], e_out[:, b, 1, :], ALU.subtract
                                    ).then_inc(s_elo, 1)
                    dve.wait_ge(s_wt, i2 + (b + 1))
                    ch.link(v.tensor_copy(w_col[:, :], misc(b)["w_t"]))
                    v.tensor_copy(weighted[:, :, 0], w_col[:, :])
                    v.tensor_tensor(weighted[:, :, 1:D + 1], rows[:, b, :, :],
                                    w_col[:, :].unsqueeze(2).to_broadcast([PART, K, D]), ALU.mult
                                    ).then_inc(s_wf, 1)
                    blk = load_blocks(dve, regs, block_row, (i * 2 + b) * K, 1)[0]
                    dve.wait_ge(s_fh, i2 + (b + 1))
                    ch.link(v.tensor_tensor(resc_col[:, :], first_hot[:, b:b + 1], misc(b)["resc"], ALU.mult))
                    ch.link(v.tensor_scalar(resc_col[:, :], resc_col[:, :], 1.0, None, ALU.add))
                    if prev:
                        dve.wait_ge(s_acc0, i32 + K * b)
                    a = agg0[:, ds(blk, 1), :]
                    ch.link(v.tensor_scalar(a, a, resc_col[:, :], None, ALU.mult))
                assert ch.n == CH0, ch.n

            ch = Chain(dve, s_pro, pro.n)
            ch.link(v.tensor_copy(relc[:, 0, :], rel[:, 0:K]))
            one_hots0(0, 0, K)
            iterations(dve, ITERS, iter0)
            part_rest(2 * ITERS, -1)
            part_lo(2 * ITERS, -1)
            at = load_blocks(dve, regs, block_row, TILES - K, K)
            accumulate0(32 * ITERS, -1, at, 0, K)
            dve.wait_ge(s_acc0, TILES)

            ln = Chain(dve, s_ln)

            def bc(a):
                return a.unsqueeze(2).to_broadcast([PART, NB, D])

            def layernorm(y, z, o, done_act):
                ln.link(v.tensor_reduce(stat[:, 0, :], y, AX.X, ALU.add))
                ln.link(v.tensor_scalar(stat[:, 0, :], stat[:, 0, :], 1.0 / D, None, ALU.mult))
                ln.link(v.tensor_tensor(y, y, bc(stat[:, 0, :]), ALU.subtract))
                ln.link(v.tensor_tensor(z, y, y, ALU.mult))
                ln.link(v.tensor_reduce(stat[:, 1, :], z, AX.X, ALU.add))
                dve.wait_ge(s_lna, done_act)
                ln.link(v.reciprocal(stat[:, 3, :], stat[:, 2, :]))
                v.tensor_tensor(o, y, bc(stat[:, 3, :]), ALU.mult).then_inc(s_x1, 1)

            ln.link(v.tensor_scalar(stat[:, 0, :], agg0[:, 0:NB, 0], 1e-30, None, ALU.max))
            ln.link(v.reciprocal(stat[:, 1, :], stat[:, 0, :]))
            ln.link(v.tensor_tensor(bulk_a, agg0[:, 0:NB, 1:D + 1], bc(stat[:, 1, :]), ALU.mult))
            ln.link(v.tensor_scalar(bulk_b, bulk_a, 0.0, None, ALU.min))
            dve.wait_ge(s_lna, 1)
            ln.link(v.scalar_tensor_tensor(bulk_a, bulk_a, 0.0, bulk_b, ALU.max, ALU.add))
            ln.link(v.scalar_tensor_tensor(bulk_a, bulk_a, -1.0, xn[:, 0:NB, :], ALU.add, ALU.add))
            v.memset(agg[:, NB:NBP, :], 0.0)
            for s in range(2):
                dve.wait_ge(s_eout[s], 16 * ITERS)
            v.memset(edge_f[96:PART, :, :, :], 1.0)
            layernorm(bulk_a, bulk_b, agg[:, 0:NB, :], 2)
            dve.wait_ge(s_x1, 1)

            def node(n):
                end = isinstance(n, int) and n == LAYERS
                if not end:
                    dve.wait_ge(s_w_in, n * 64 + 64)
                    we = Chain(dve, s_we, held(dve, n * N_WE))
                    part = [w_e_part[:, s, :] for s in range(3)]
                    we.link(v.tensor_copy(part[0], w_e_sb[:, :]))
                    we.link(v.tensor_tensor(w_e_rest[:, :], w_e_sb[:, :], part[0], ALU.subtract))
                    we.link(v.tensor_copy(part[1], w_e_rest[:, :]))
                    we.link(v.tensor_tensor(part[2], w_e_rest[:, :], part[1], ALU.subtract))
                    we.link(v.tensor_scalar(w_e_rest[:, :], part[0], mask[:, 0:1], None, ALU.mult))
                    we.link(v.scalar_tensor_tensor(w_e_rest[:, :], part[1], mask[:, 1:2], w_e_rest[:, :],
                                                   ALU.mult, ALU.add))
                    we.link(v.scalar_tensor_tensor(w_e7[:, :], part[2], mask[:, 2:3], w_e_rest[:, :],
                                                   ALU.mult, ALU.add))
                    assert we.n == N_WE
                else:
                    dve.wait_ge(s_x1d, 32)

                def group(i, first):
                    g5 = held(dve, (n * GI + i) * GU)
                    g15 = held(dve, g5 * 3)
                    for u in range(GU):
                        v.tensor_copy(stage[:, u, :, :], agg[:, ds((i * GU + u) * GB, GB), :]).then_inc(s_st, 1)
                    for u in range(GU):
                        if end:
                            dve.wait_ge(s_back, held(dve, i * GU) + (u + 1))
                            y = p3_raw[:, ds((i * GU + u) * (GB * D), GB * D)]
                            v.tensor_tensor(y, y, ps[:, 4 + u % 4, 0:GB * D], ALU.add).then_inc(s_fin, 1)
                            continue
                        dve.wait_ge(s_qc, g5 + (u + 1))
                        p_f = stage_pq[:, u, :, 0:D]
                        at = (i * GU + u) * GB
                        part = [p3[:, ds(at * PW, GB * PW)].rearrange("p (b w) -> p b w", w=PW)[:, :, s * D:(s + 1) * D]
                                for s in range(3)]
                        v.tensor_copy(part[0], p_f).then_inc(s_split, 1)
                        dve.wait_ge(s_split, g15 + (3 * u + 1))
                        v.tensor_tensor(p_rest[:, :, :], p_f, part[0], ALU.subtract).then_inc(s_split, 1)
                        dve.wait_ge(s_split, g15 + (3 * u + 2))
                        v.tensor_copy(part[1], p_rest[:, :, :]).then_inc(s_split, 1)
                        dve.wait_ge(s_split, g15 + (3 * u + 3))
                        v.tensor_tensor(part[2], p_rest[:, :, :], part[1], ALU.subtract).then_inc(s_p3, 1)
                iterations(dve, GI, group)

            def edge(layer):
                def take(c, g2, i):
                    v.tensor_copy(relc[:, c % 2, :], rel[:, ds((i * 2 + c) * K, K)]).then_inc(s_relc, 1)
                    dve.wait_ge(s_relc, g2 + (c + 1))

                def prepare(q, at, lo, hi):
                    b, h = q // 2 % 2, q % 2
                    for t in range(lo, hi):
                        c = h * H + t
                        v.tensor_copy(win[:, H * h + t, :], p3[:, ds(at[t] * PW, 2 * PW)])
                        v.tensor_scalar(hot[:, K * b + c, :], iota[:, :], relc[:, b, c:c + 1], None,
                                        ALU.is_equal).then_inc(s_hot, 1)

                def accumulate(g32, q, at, lo, hi, start=False):
                    for t in range(lo, hi):
                        tau = H * q + t
                        dve.wait_ge(s_aggm, g32 + (tau - t + (t | 1) + 1))
                        if not (start and t == 0):
                            dve.wait_ge(s_acc, g32 + tau)
                        a = agg[:, ds(at[t], 2), :]
                        v.tensor_tensor(a, a, agg_slot(tau)[:, :, 0:D], ALU.add).then_inc(s_acc, 1)

                def rest(g4, q):
                    m = rows[:, q // 2 % 2, q % 2 * H:q % 2 * H + H, :]
                    dve.wait_ge(s_hi, g4 + (q + 1))
                    v.scalar_tensor_tensor(m, m, 0.0, msg[:, q % 2, 0, :, :], ALU.max, ALU.subtract
                                           ).then_inc(s_rest, 1)

                def low(g4, q):
                    m = rows[:, q // 2 % 2, q % 2 * H:q % 2 * H + H, :]
                    dve.wait_ge(s_mid, g4 + (q + 1))
                    v.tensor_tensor(msg[:, q % 2, 2, :, :], m, msg[:, q % 2, 1, :, :], ALU.subtract
                                    ).then_inc(s_lo[q % 4], 1)

                def halves(i, first):
                    g = held(dve, layer * ITERS + i)
                    g32, g16, g4 = held(dve, g * 32), held(dve, g * 16), held(dve, g * 4)
                    r2 = held(dve, layer * (2 * ITERS + 1) + i * 2)
                    for q in range(4):
                        b, h = q // 2, q % 2
                        lag1, lag2 = not (first and q == 0), not (first and q < 2)
                        nxt = load_blocks(dve, regs[:H], block_row, (i * 4 + q + 1) * H, H)
                        if h == 1:
                            take(b + 1, r2, i)
                        prepare(q + 1, nxt, 0, 2)
                        if lag1:
                            rest(g4, q - 1)
                        prepare(q + 1, nxt, 2, 4)
                        if lag1:
                            low(g4, q - 1)
                        prepare(q + 1, nxt, 4, 6)
                        if lag2:
                            old = load_blocks(dve, regs[K:K + H], block_row, (i * 4 + q - 2) * H, H)
                            accumulate(g32, q - 2, old, 0, 4, start=first and q == 2)
                        prepare(q + 1, nxt, 6, 8)
                        if lag2:
                            accumulate(g32, q - 2, old, 4, 8)
                        dve.wait_ge(s_pre, g16 + 4 * (q + 1))
                        dve.wait_ge(s_rows[b][h], g * 128 + 128)
                        m = rows[:, b, h * H:h * H + H, :]
                        v.tensor_tensor(m, m, pre_bank(q), ALU.add).then_inc(s_add, 1)

                for u in range(GU):
                    dve.wait_ge(s_qt[u], layer * (16 * GI) + 16 * GI)
                dve.wait_ge(s_zero, layer * PH + PH)
                hold_waits(dve, s_past[2])
                nxt = load_blocks(dve, regs[:H], block_row, 0, H)
                take(0, held(dve, layer * (2 * ITERS + 1)), 0)
                prepare(0, nxt, 0, H)
                iterations(dve, ITERS, halves)
                g4 = held(dve, layer * (4 * ITERS) + 4 * ITERS)
                g32 = held(dve, layer * TILES + TILES)
                rest(g4, -1)
                low(g4, -1)
                for q in (-2, -1):
                    old = load_blocks(dve, regs[K:K + H], block_row, TILES + q * H, H)
                    accumulate(g32, q, old, 0, H)
                dve.wait_ge(s_acc, g32)

            phases(dve, node, edge)

            dve.wait_ge(s_fin, PH)
            ln.n += 1
            v.memset(resc[:, :], 0.0).then_inc(s_ln, 1)
            layernorm(bulk_b, bulk_a, agg[:, 0:NB, :], 3)


def dst_rows(dst_flat, at):
    row = dst_flat[0:1, bass.ds(at, K * PART + 2)]
    return bass.AP(tensor=row.tensor, offset=row.offset, ap=[[PART, K], [1, PART + 2]])


def hold_waits(engine, past):
    engine.sem_inc(past, 1)


def load_blocks(engine, regs, block_row, at, n):
    engine.load(regs[:n], block_row[0:1, bass.ds(at, n)])
    return [engine.snap(r, min_val=0, max_val=NB - 1) for r in regs[:n]]


_OUT = ((N, D), "float32")


def kernel(x, src, dst, edge_attr_16, L0_gnn_attn_l, L0_gnn_attn_r, L1_gnn_msg_w, L1_gnn_msg_b,
           L1_gnn_upd_w, L1_gnn_upd_b):
    import concourse.bacc as bacc
    from concourse.bass_utils import run_bass_kernel_spmd

    src, dst, ef = np.asarray(src), np.asarray(dst), np.asarray(edge_attr_16)
    pad = TILES * PART - E
    src_p = np.concatenate([src, np.zeros(pad, src.dtype)])
    dst_p = np.concatenate([dst, np.full(pad, NB * PART - 1, dst.dtype)])
    tiles = dst_p.reshape(TILES, PART)
    mw, uw = np.asarray(L1_gnn_msg_w), np.asarray(L1_gnn_upd_w)
    mb, ub = np.asarray(L1_gnn_msg_b), np.asarray(L1_gnn_upd_b)
    none = np.zeros((1, PART, D), mw.dtype)
    w_e = np.zeros((LAYERS, PART, D), mw.dtype)
    w_e[:, 0:7 * DE] = np.tile(mw[:, 2 * D:], (1, 7, 1))
    w_e[:, 7 * DE:KE] = mb[:, None]
    masks = np.zeros((PART, 3), np.float32)
    for part in range(3):
        masks[32 * part:32 * part + 32, part] = 1
        masks[7 * DE + part, part] = 1
    masks[6 * DE:7 * DE, 0] = 1
    arrays = {
        "x": np.asarray(x),
        "src_cols": src_p.reshape(TILES, PART).T,
        "dst_cols": tiles.T,
        "dst_flat": np.concatenate([np.full(1, -1, dst.dtype), dst_p, np.full(1, -1, dst.dtype)])[None],
        "dst_first": tiles[:, 0][None],
        "dst_last": tiles[:, -1][None],
        "edge_t": np.concatenate([ef, np.zeros((pad, DE), ef.dtype)]).T,
        "attn_l": np.asarray(L0_gnn_attn_l)[None],
        "attn_r": np.asarray(L0_gnn_attn_r)[None],
        "w_ij": np.concatenate([np.concatenate([mw[:, 0:D], mw[:, D:2 * D]], axis=2), none[:, 0:D].repeat(2, 2)]
                               ).reshape((LAYERS + 1) * D, 2 * D),
        "w_e": np.concatenate([w_e, none]).reshape((LAYERS + 1) * PART, D),
        "w_u": np.concatenate([none, uw]).reshape((LAYERS + 1) * PART, D),
        "b_u": np.concatenate([np.zeros((1, D), ub.dtype), ub]).reshape((LAYERS + 1) * D, 1),
        "masks": masks,
    }
    arrays = {k: np.ascontiguousarray(a) for k, a in arrays.items()}
    nc = bacc.Bacc("TRN2", target_bir_lowering=False, num_devices=1)
    args = {k: nc.dram_tensor(f"in_{k}", a.shape, mybir.dt.from_np(a.dtype), kind="ExternalInput").ap()
            for k, a in arrays.items()}
    out = nc.dram_tensor("out_0", _OUT[0], F32, kind="ExternalOutput").ap()
    build(nc, out=out, **args)
    result = run_bass_kernel_spmd(nc, [{f"in_{k}": a for k, a in arrays.items()}], core_ids=[0])
    return result.results[0]["out_0"]
```

```python
from contextlib import ExitStack

import numpy as np

import concourse.bass as bass
from concourse import mybir
from concourse.bass import IndirectOffsetOnAxis

F32 = mybir.dt.float32
BF16 = mybir.dt.bfloat16
I32 = mybir.dt.int32
ALU = mybir.AluOpType
ACT = mybir.ActivationFunctionType
AX = mybir.AxisListType

N, D = 12500, 64
E, DE = 212500, 16
LAYERS = 3
PART = 128
K = 16
H = K // 2
TILES = -(-E // (2 * K * PART)) * 2 * K
ITERS = TILES // (2 * K)
NB = -(-N // PART)
GB = 4
GU = 5
GI = -(-(NB + 1) // (GB * GU))
NBP = GI * GU * GB
NT = NB - 1
NREST = N - NT * PART
BIG = 2.0 ** 126
EPS = 1e-5
SLOPE = 0.2
PW = 3 * D
KE = 3 * DE + 3
WR = 64
N_WE = 9


class Chain:

    def __init__(self, engine, sem, base=0):
        self.engine, self.sem, self.base, self.n = engine, sem, base, 0

    def mark(self, ins):
        self.n += 1
        ins.then_inc(self.sem, 1)

    def join(self):
        self.engine.wait_ge(self.sem, self.base + self.n)

    def link(self, ins):
        self.mark(ins)
        self.join()


def held(engine, value):
    return value if isinstance(value, int) else engine.snap(value)


def build(nc, x, src_cols, dst_cols, dst_flat, dst_first, dst_last, edge_t, attn_l, attn_r,
          w_ij, w_e, w_u, b_u, masks, out):
    ds = bass.ds
    ctx = ExitStack()
    with ctx:
        def sb(name, shape, dt=F32):
            return ctx.enter_context(nc.sbuf_tensor(name, shape, dt))

        def sem(name):
            return ctx.enter_context(nc.semaphore(name))

        q_table = nc.dram_tensor("q_table", (NBP * PART, D), F32).ap()
        x_ext = nc.dram_tensor("x_ext", (NB * PART, D + 2), F32).ap()
        x1_dram = nc.dram_tensor("x1_dram", (PART, NB * D), F32).ap()
        e_parts = nc.dram_tensor("e_parts", (3 * DE, TILES * PART), BF16).ap()

        xs_t = sb("xs_t", [PART, NBP * PART])
        FT = TILES + K + 1
        NH = -(-NB // 2)
        AT1 = max(2 * FT, NH * D)
        p3_raw = sb("p3_raw", [PART, max(NBP * PW // 2, AT1 + NBP * (D + 1))])
        p3 = p3_raw[:, :].bitcast(BF16)
        agg_raw = sb("agg_raw", [PART, NBP * (D + 1)])
        rows_raw = sb("rows_raw", [PART, 2 * K * (D + 2)])
        n_hot = 2 * K * 2 * PART // 2
        n_win = 2 * H * 2 * PW // 2
        n_msg = 2 * 3 * H * D // 2
        shared = sb("shared", [PART, max(n_hot + n_win + n_msg, NB * D)])
        weighted = sb("weighted", [PART, K, D + 1])
        rel = sb("rel", [PART, TILES + K], BF16)
        relc = sb("relc", [PART, 2, K])
        idx = sb("idx", [PART, 2, K], I32)
        edge_f = sb("edge_f", [WR, 2, K, PART], BF16)
        block_row = sb("block_row", [1, TILES + K], I32)
        hot_t = sb("hot_t", [PART, 2, 2, 2 * PART], BF16)
        iota_i = sb("iota_i", [PART, 2 * PART], I32)
        iota = sb("iota", [PART, 2 * PART], BF16)
        pidx_i = sb("pidx_i", [PART, 1], I32)
        pidx = sb("pidx", [PART, 1])
        ident = sb("ident", [PART, PART])
        ident_b = sb("ident_b", [PART, PART], BF16)
        ones = sb("ones", [1, PART])
        zeros = sb("zeros", [PART, GB, D])
        eps = sb("eps", [PART, 1])
        al = sb("al", [PART, D])
        ar = sb("ar", [PART, D])
        er = sb("er", [PART, NBP])
        er_rest = sb("er_rest", [PART, NBP])
        er_win = sb("er_win", [PART, 2, K, 6], BF16)
        er3 = sb("er3", [PART, NBP, 3], BF16)
        x_t_raw = sb("x_t_raw", [PART, GU * GB * PART])
        w_ij_sb = sb("w_ij_sb", [D, 2 * D])
        w_e_sb = sb("w_e_sb", [WR, D])
        w_e_rest = sb("w_e_rest", [WR, D])
        w_e_part = sb("w_e_part", [WR, 3, D], BF16)
        w_e3 = sb("w_e3", [WR, 3, D], BF16)
        w_u_sb = sb("w_u_sb", [PART, D])
        b_u_sb = sb("b_u_sb", [D, 1])
        mask = sb("mask", [WR, 4])
        p_rest = sb("p_rest", [PART, GB, D])
        ere = sb("ere", [PART, K])
        ec = sb("ec", [PART, K])
        e_row = sb("e_row", [K, PART])
        dst_row = sb("dst_row", [K, 2, PART + 2], I32)
        same = sb("same", [K, PART + 1])
        fwd = sb("fwd", [K, PART])
        bwd = sb("bwd", [K, PART])
        fwd_chain = sb("fwd_chain", [1, 2, K + 1])
        bwd_chain = sb("bwd_chain", [1, K + 1])
        carry_row = sb("carry_row", [1, 2 * K])
        carry_col = sb("carry_col", [K, 2])
        shift = sb("shift", [K, PART])
        w_row = sb("w_row", [K, PART])
        w_col = sb("w_col", [PART, K])
        resc = sb("resc", [1, 2])
        first_hot = sb("first_hot", [PART, 2])
        resc_col = sb("resc_col", [PART, 1])
        stat = sb("stat", [PART, 4, NBP])

        er3_f = er3[:, :, :].rearrange("p b s -> p (b s)")

        hot = shared[:, 0:n_hot].bitcast(BF16).rearrange("p (t n) -> p t n", n=2 * PART)
        win = shared[:, n_hot:n_hot + n_win].bitcast(BF16).rearrange("p (t w) -> p t w", w=2 * PW)
        msg = shared[:, n_hot + n_win:n_hot + n_win + n_msg].bitcast(BF16).rearrange(
            "p (q s t d) -> p q s t d", q=2, s=3, d=D)
        n_wt = 3 * K * (D + 1) // 2
        wparts = shared[:, n_hot:n_hot + 2 * n_wt].bitcast(BF16).rearrange(
            "p (b s t d) -> p b s t d", b=2, s=3, d=D + 1)
        n_st = GU * GB * D
        stage = shared[:, 0:n_st].rearrange("p (u b d) -> p u b d", u=GU, b=GB)
        stage_pq = shared[:, n_st:3 * n_st].rearrange("p (u b d) -> p u b d", u=GU, b=GB)
        bulk_a = shared[:, 0:NB * D].rearrange("p (b d) -> p b d", d=D)
        bulk_b = p3_raw[:, 0:NB * D].rearrange("p (b d) -> p b d", d=D)
        rows = rows_raw[:, 0:2 * K * D].rearrange("p (b t d) -> p b t d", b=2, t=K)
        x_t = x_t_raw[0:D, :].rearrange("p (u n) -> p u n", u=GU)
        agg0 = agg_raw[:, :].rearrange("p (b d) -> p b d", d=D + 1)
        agg1 = p3_raw[:, AT1:AT1 + NBP * (D + 1)].rearrange("p (b d) -> p b d", d=D + 1)
        agg = agg_raw[:, 0:NBP * D].rearrange("p (b d) -> p b d", d=D)
        rows0 = rows_raw[:, :].rearrange("p (b t d) -> p b t d", b=2, t=K)
        xe = xs_t[:, 0:NB * (D + 2)].rearrange("p (b d) -> p b d", d=D + 2)
        xn = xe[:, :, 1:D + 1]
        flags = p3[0:1, 0:4 * FT].rearrange("p (f t) -> p f t", f=4)
        EW = DE * K
        e_in = x_t_raw[:, 0:2 * EW].rearrange("p (b e) -> p b e", b=2)
        e_out = x_t_raw[:, 2 * EW:5 * EW].bitcast(BF16).rearrange("p (b s e) -> p b s e", b=2, s=3)
        e_rest = x_t_raw[:, 5 * EW:7 * EW].rearrange("p (b e) -> p b e", b=2)
        ints = shared[:, :].bitcast(I32)
        dst_c_i = ints[:, 0:TILES]
        first_b_i = ints[:, TILES:2 * TILES]
        first_i = ints[0:1, 2 * TILES:3 * TILES]
        last_i = ints[0:1, 3 * TILES:4 * TILES]

        ps = ctx.enter_context(nc.psum_tensor("ps", [PART, 8, 512], F32))

        def t_bank(pair):
            return ps[:, pair % 2, 0:256].bitcast(BF16)

        def pre_bank(half):
            return ps[:, 2 + half % 2, :].rearrange("p (t d) -> p t d", d=D)

        def agg_slot(tile):
            return ps[:, 4 + tile % 4 // 2, 256 * (tile % 2):256 * (tile % 2) + 256].rearrange(
                "p (j d) -> p j d", j=2)

        def er_bank(b):
            return ps[:, 2 + b, 0:3 * K].rearrange("p (t s) -> p t s", s=3)

        def misc(b):
            m = ps[:, 6 + b, :]
            return {"e_t": m[0:K, 0:PART], "ends": m[0:1, 128:128 + 2 * K], "carry": m[0:K, 160:162],
                    "w_t": m[:, 192:192 + K], "resc": m[:, 224:225]}

        s_in = sem("s_in")
        s_xin = [sem(f"s_xin{h}") for h in range(2)]
        s_el = sem("s_el")
        s_xe = sem("s_xe")
        s_iota = sem("s_iota")
        s_const = sem("s_const")
        s_pro = sem("s_pro")
        s_past = [sem(f"s_past_{e}") for e in ("pool", "pe", "dve", "act", "sp")]
        s_idx = [sem(f"s_idx{b}") for b in range(2)]
        s_dstrow = [sem(f"s_dstrow{b}") for b in range(2)]
        s_ein = [sem(f"s_ein{b}") for b in range(2)]
        s_eout = [sem(f"s_eout{b}") for b in range(2)]
        s_ehi, s_erest, s_emid, s_elo = (sem(f"s_e_{k}") for k in ("hi", "rest", "mid", "lo"))
        s_rows0 = [sem(f"s_rows0_{b}") for b in range(2)]
        s_hot0 = sem("s_hot0")
        s_t0 = sem("s_t0")
        s_tc0 = sem("s_tc0")
        s_win = sem("s_win")
        s_fh = sem("s_fh")
        s_er = sem("s_er")
        s_ec = sem("s_ec")
        s_et = sem("s_et")
        s_ends = sem("s_ends")
        s_endst = sem("s_endst")
        s_carry = sem("s_carry")
        s_carryt = sem("s_carryt")
        s_shift = sem("s_shift")
        s_diff = sem("s_diff")
        s_w = sem("s_w")
        s_resc = sem("s_resc")
        s_wt = sem("s_wt")
        s_wf = sem("s_wf")
        s_whi, s_wrest, s_wmid, s_wlo = (sem(f"s_w_{k}") for k in ("hi", "rest", "mid", "lo"))
        s_aggm0 = sem("s_aggm0")
        s_acc0 = sem("s_acc0")
        s_ch0 = sem("s_ch0")
        s_ln = sem("s_ln")
        s_lna = sem("s_lna")
        s_x1 = sem("s_x1")
        s_x1d = sem("s_x1d")
        s_nm = sem("s_nm")
        s_nma = sem("s_nma")
        s_res = sem("s_res")
        s_w_in = sem("s_w_in")
        s_we = sem("s_we")
        s_st = sem("s_st")
        s_zero = sem("s_zero")
        s_tr = sem("s_tr")
        s_ca = sem("s_ca")
        s_up = sem("s_up")
        s_rl = sem("s_rl")
        s_keep = sem("s_keep")
        s_pq = sem("s_pq")
        s_qc = sem("s_qc")
        s_split = sem("s_split")
        s_p3 = sem("s_p3")
        s_qt = [sem(f"s_qt{u}") for u in range(GU)]
        s_back = sem("s_back")
        s_fin = sem("s_fin")
        s_rows = [[sem(f"s_rows_{b}{h}") for h in range(2)] for b in range(2)]
        s_edge = [sem(f"s_edge{b}") for b in range(2)]
        s_relc = sem("s_relc")
        s_hot = sem("s_hot")
        s_t = sem("s_t")
        s_tc = sem("s_tc")
        s_pre = sem("s_pre")
        s_add = sem("s_add")
        s_hi, s_rest, s_mid = sem("s_hi"), sem("s_rest"), sem("s_mid")
        s_lo = [sem(f"s_lo{q}") for q in range(4)]
        s_aggm = sem("s_aggm")
        s_acc = sem("s_acc")
        s_out = sem("s_out")
        block = ctx.enter_context(nc.Block())

        N_XIN, N_IN = 3, 5
        CH0 = 42
        N_NM = 6
        PH = GI * GU

        def phases(engine, node, edge):
            node(0)
            with engine.Fori(0, LAYERS - 1) as layer:
                edge(layer)
                node(layer + 1)
            edge(LAYERS - 1)
            node(LAYERS)

        def iterations(engine, n, body):
            body(0, True)
            if n > 1:
                with engine.Fori(1, n) as i:
                    body(i, False)

        @block.sync
        def _(sp):
            for u in range(GU):
                sp.sem_inc(s_qt[u], 16)
            sp.dma_start(al[:, :], attn_l.partition_broadcast(PART)).then_inc(s_xin[0], 16)
            sp.dma_start(ar[:, :], attn_r.partition_broadcast(PART)).then_inc(s_xin[0], 16)
            x_b = x[0:NT * PART, :].rearrange("(b p) d -> p b d", p=PART)
            sp.dma_start(xn[:, 0:NH, :], x_b[:, 0:NH, :]).then_inc(s_xin[0], 16)
            sp.dma_start(xn[:, NH:NT, :], x_b[:, NH:NT, :]).then_inc(s_xin[1], 16)
            sp.dma_start(xn[0:NREST, NT, :], x[NT * PART:N, :]).then_inc(s_xin[1], 16)
            sp.dma_start(xn[NREST:PART, NT, :], x[0:PART - NREST, :]).then_inc(s_xin[1], 16)
            sp.dma_start(dst_c_i, dst_cols).then_inc(s_in, 16)
            sp.dma_start(first_b_i, dst_first.partition_broadcast(PART)).then_inc(s_in, 16)
            sp.dma_start(first_i, dst_first).then_inc(s_in, 16)
            sp.dma_start(last_i, dst_last).then_inc(s_in, 16)
            sp.dma_start(mask[:, :], masks).then_inc(s_in, 16)

            e_flat = edge_t.rearrange("f (k e) -> (f k) e", k=PART // DE)
            p_flat = e_parts.rearrange("(s f) (k e) -> (f k) s e", s=3, k=PART // DE)

            def load0(i, first):
                for b in range(2):
                    if not first:
                        sp.wait_ge(s_rows0[b], i * (16 * K))
                    sp.dma_start(idx[:, b, :], src_cols[:, ds((i * 2 + b) * K, K)]).then_inc(s_idx[b], 16)
                    if not first:
                        sp.wait_ge(s_shift, i * 2 + (b - 1))
                    sp.dma_start(dst_row[:, b, :], dst_rows(dst_flat, (i * 2 + b) * (K * PART))
                                 ).then_inc(s_dstrow[b], 16)
                    if not first:
                        sp.wait_ge(s_erest, i * 2 + (b - 1))
                    sp.dma_start(e_in[:, b, :], e_flat[:, ds((i * 2 + b) * EW, EW)]).then_inc(s_ein[b], 16)
                    if not first:
                        store_parts(i - 1, b)

            def store_parts(i, b):
                at = held(sp, (i * 2 + b) * EW)
                sp.wait_ge(s_elo, i * 2 + (b + 1))
                hold_waits(sp, s_past[4])
                sp.dma_start(p_flat[:, :, ds(at, EW)], e_out[:, b, :, :]).then_inc(s_eout[b], 16)

            def load_weights(n):
                sp.dma_start(w_ij_sb[:, :], w_ij[ds(n * D, D), :]).then_inc(s_w_in, 16)
                sp.dma_start(w_e_sb[:, :], w_e[ds(n * WR, WR), :]).then_inc(s_w_in, 16)
                sp.dma_start(w_u_sb[:, :], w_u[ds(n * PART, PART), :]).then_inc(s_w_in, 16)
                sp.dma_start(b_u_sb[:, :], b_u[ds(n * D, D), :]).then_inc(s_w_in, 16)

            load_weights(0)
            table = x_ext.rearrange("(b p) d -> p b d", p=PART)
            for h, (lo, hi) in enumerate(((0, NH), (NH, NB))):
                sp.wait_ge(s_el, h + 1)
                sp.dma_start(table[:, lo:hi, :], xe[:, lo:hi, :]).then_inc(s_xe, 16)
            iterations(sp, ITERS, load0)
            for b in range(2):
                store_parts(ITERS - 1, b)

            sp.wait_ge(s_iota, 2)
            sp.wait_ge(s_x1, 1)
            sp.dma_start(x1_dram, agg_raw[:, 0:NB * D]).then_inc(s_x1d, 16)
            for b in range(2):
                sp.wait_ge(s_eout[b], 16 * ITERS)

            def node(n):
                if isinstance(n, int) and n == LAYERS:
                    sp.wait_ge(s_acc, LAYERS * TILES)
                    sp.dma_start(p3_raw[:, 0:NB * D], x1_dram).then_inc(s_x1d, 16)
                    return
                rows_q = q_table.rearrange("(b p) d -> p b d", p=PART)

                def store_q(i, first):
                    g5 = held(sp, (n * GI + i) * GU)
                    for u in range(GU):
                        sp.wait_ge(s_qc, g5 + (u + 1))
                        sp.dma_start(rows_q[:, ds((i * GU + u) * GB, GB), :], stage_pq[:, u, :, D:2 * D]
                                     ).then_inc(s_qt[u], 16)
                iterations(sp, GI, store_q)
                sp.wait_ge(s_p3, n * PH + (PH + GU))
                load_weights(n + 1)

            def edge(layer):
                def load(i, first):
                    g = held(sp, layer * ITERS + i)
                    for b in range(2):
                        if not first:
                            for h in range(2):
                                sp.wait_ge(s_rows[b][h], g * (16 * H))
                        sp.dma_start(idx[:, b, :], src_cols[:, ds((i * 2 + b) * K, K)]).then_inc(s_idx[b], 16)
                        if not first:
                            sp.wait_ge(s_pre, g * 16 + (8 * b - 8))
                        cols = ds((i * 2 + b) * (K * PART), K * PART)
                        sp.dma_start(edge_f[0:3 * DE, b, :, :].rearrange("p t e -> p (t e)"), e_parts[:, cols]
                                     ).then_inc(s_edge[b], 16)
                iterations(sp, ITERS, load)

            phases(sp, node, edge)

            nb = GU * GB
            out_b = out[0:NT * PART, :].rearrange("(b p) d -> p b d", p=PART)
            for i in range(GI):
                sp.wait_ge(s_res, i + 1)
                hi = min((i + 1) * nb, NT)
                sp.dma_start(out_b[:, i * nb:hi, :], agg[:, i * nb:hi, :]).then_inc(s_out, 16)
            sp.dma_start(out[NT * PART:N, :], agg[0:NREST, NT, :]).then_inc(s_out, 16)
            sp.wait_ge(s_out, 16 * (GI + 1))

        @block.gpsimd
        def _(pool):
            nc.gpsimd.iota(iota_i[:, :], [[1, 2 * PART]], base=0, channel_multiplier=0)
            nc.gpsimd.iota(pidx_i[:, :], [[1, 1]], base=0, channel_multiplier=1).then_inc(s_iota, 1)
            pool.wait_ge(s_iota, 1)
            nc.gpsimd.memset(edge_f[32:WR, :, :, :], 1.0).then_inc(s_iota, 1)

            def gather(dest, table, b, lo, hi, s):
                for t in range(lo, hi):
                    nc.gpsimd.indirect_dma_start(
                        dest[:, b, t, :], None, table,
                        IndirectOffsetOnAxis(ap=idx[:, b, t:t + 1], axis=0)).then_inc(s, 16)

            def gather0(i, first):
                for b in range(2):
                    pool.wait_ge(s_idx[b], i * 16 + 16)
                    if not first:
                        pool.wait_ge(s_wf, i * 2 + (b - 1))
                    hold_waits(pool, s_past[0])
                    gather(rows0, x_ext, b, 0, K, s_rows0[b])
            pool.wait_ge(s_iota, 2)
            pool.wait_ge(s_xe, 32)
            iterations(pool, ITERS, gather0)

            def node(n):
                last = isinstance(n, int) and n == LAYERS
                if last:
                    return
                if isinstance(n, int) and n == 0:
                    pool.wait_ge(s_x1d, 16)

                def group(i, first):
                    g5 = held(pool, (n * GI + i) * GU)
                    for u in range(GU):
                        pool.wait_ge(s_st, g5 + (u + 1))
                        hold_waits(pool, s_past[0])
                        nc.gpsimd.tensor_copy(agg[:, ds((i * GU + u) * GB, GB), :], zeros[:, :, :]
                                              ).then_inc(s_zero, 1)
                    for u in range(GU):
                        pool.wait_ge(s_rl, g5 + (u + 1))
                        hold_waits(pool, s_past[0])
                        nc.gpsimd.tensor_copy(xs_t[0:D, ds((i * GU + u) * (GB * PART), GB * PART)], x_t[:, u, :]
                                              ).then_inc(s_keep, 1)
                iterations(pool, GI, group)

            def edge(layer):
                for u in range(GU):
                    pool.wait_ge(s_qt[u], layer * (16 * GI) + 16 * (GI + 1))
                hold_waits(pool, s_past[0])

                def gathers(i, first):
                    g = held(pool, layer * ITERS + i)
                    for b in range(2):
                        for h in range(2):
                            if h == 0:
                                pool.wait_ge(s_idx[b], g * 16 + (16 * ITERS + 16))
                            if not first:
                                pool.wait_ge(s_lo[2 * b + h], g)
                            if h == 0 or not first:
                                hold_waits(pool, s_past[0])
                            gather(rows, q_table, b, h * H, h * H + H, s_rows[b][h])
                iterations(pool, ITERS, gathers)

            phases(pool, node, edge)

        @block.scalar
        def _(act):
            regs = [act.alloc_register(f"tile_block{k}") for k in range(K)]
            act.wait_ge(s_const, 1)

            def copy_pairs(base16, c, lo, hi):
                for k in range(lo, hi):
                    p = 8 * c + k
                    act.wait_ge(s_t0, base16 + (p + 1))
                    if not (isinstance(base16, int) and base16 + p < 2):
                        act.wait_ge(s_er, base16 + (p - 1))
                    if k == 0:
                        nc.scalar.copy(first_hot[:, c % 2:c % 2 + 1], t_bank(p)[:, 0:1]).then_inc(s_fh, 1)
                    nc.scalar.copy(hot_t[:, p % 2, :, :].rearrange("p a b -> p (a b)"), t_bank(p)
                                   ).then_inc(s_tc0, 1)

            def windows(at, c):
                blocks = load_blocks(act, regs, block_row, at, K)
                for t in range(K):
                    last = nc.scalar.copy(er_win[:, c % 2, t, :], er3_f[:, ds(blocks[t] * 3, 6)])
                last.then_inc(s_win, 1)

            def hi0(i2, c):
                act.wait_ge(s_wf, i2 + (c + 1))
                nc.scalar.copy(wparts[:, c % 2, 0, :, :], weighted[:, :, :]).then_inc(s_whi, 1)

            def mid0(i2, c):
                act.wait_ge(s_wrest, i2 + (c + 1))
                nc.scalar.copy(wparts[:, c % 2, 1, :, :], weighted[:, :, :]).then_inc(s_wmid, 1)

            def iter0(i, first):
                i16, i2 = held(act, i * 16), held(act, i * 2)
                for b in range(2):
                    act.wait_ge(s_ein[b], i * 16 + 16)
                    if not first:
                        act.wait_ge(s_eout[b], i * 16)
                    nc.scalar.copy(e_out[:, b, 0, :], e_in[:, b, :]).then_inc(s_ehi, 1)
                    if not (first and b == 0):
                        mid0(i2, b - 1)
                    windows((i * 2 + b + 1) * K, b + 1)
                    copy_pairs(i16, b + 1, 0, 4)
                    act.wait_ge(s_erest, i2 + (b + 1))
                    nc.scalar.copy(e_out[:, b, 1, :], e_rest[:, b, :]).then_inc(s_emid, 1)
                    act.wait_ge(s_shift, i2 + (b + 1))
                    nc.scalar.activation(w_row[:, :], shift[:, :], ACT.Exp).then_inc(s_w, 1)
                    act.wait_ge(s_diff, i2 + (b + 1))
                    nc.scalar.activation(resc[:, 1:2], resc[:, 0:1], ACT.Exp).then_inc(s_resc, 1)
                    copy_pairs(i16, b + 1, 4, 8)
                    hi0(i2, b)

            windows(0, 0)
            copy_pairs(0, 0, 0, 8)
            iterations(act, ITERS, iter0)
            mid0(2 * ITERS, -1)

            def root(n):
                act.wait_ge(s_ln, n)
                nc.scalar.activation(stat[:, 2, 0:NB], stat[:, 1, 0:NB], ACT.Sqrt, bias=eps[:, :],
                                     scale=1.0 / D).then_inc(s_lna, 1)

            act.wait_ge(s_ln, 5)
            nc.scalar.activation(bulk_b, bulk_b, ACT.Exp).then_inc(s_lna, 1)
            root(12)

            def norm_root(i):
                act.wait_ge(s_nm, held(act, i * N_NM) + 5)
                nc.scalar.activation(stat[:, 2, 0:GU * GB], stat[:, 1, 0:GU * GB], ACT.Sqrt, bias=eps[:, :],
                                     scale=1.0 / D).then_inc(s_nma, 1)

            def node(n):
                fresh = isinstance(n, int) and n == 0
                end = isinstance(n, int) and n == LAYERS

                def turned(i, first, g5, u):
                    act.wait_ge(s_tr, g5 + (u + 1))
                    t = ps[0:D, u % 2, :]
                    if fresh:
                        if not first:
                            act.wait_ge(s_keep, g5 + (u + 1 - GU))
                        nc.scalar.copy(x_t[:, u, :], t).then_inc(s_rl, 1)
                    else:
                        hold_waits(act, s_past[3])
                        nc.scalar.copy(xs_t[D:2 * D, ds((i * GU + u) * (GB * PART), GB * PART)], t
                                       ).then_inc(s_ca, 1)

                def relu(first, g5, e):
                    u = e % GU
                    act.wait_ge(s_up, g5 + (e + 1) - PH)
                    if not first and not end:
                        act.wait_ge(s_keep, g5 + (e + 1 - GU))
                    nc.scalar.activation(x_t[:, u, :], ps[0:D, 2 + u % 2, :], ACT.Relu, bias=b_u_sb[:, :]
                                         ).then_inc(s_rl, 1)

                def copy_pq(i, first, g5, e):
                    u = e % GU
                    act.wait_ge(s_pq, g5 + (e + 1))
                    if not first:
                        act.wait_ge(s_qt[u], (n * GI + i + (e // GU + 1)) * 16)
                        act.wait_ge(s_p3, g5 + (e + 1))
                    nc.scalar.copy(stage_pq[:, u, :, :].rearrange("p b d -> p (b d)"), ps[:, 4 + u % 4, :]
                                   ).then_inc(s_qc, 1)

                def lagging(i, first, g5, u):
                    if not fresh and not (first and u < 1) and u < GU + 1:
                        relu(first, g5, u - 1)
                    if not end and not (first and u < 2):
                        copy_pq(i, first, g5, u - 2)

                def group(i, first):
                    g5 = held(act, (n * GI + i) * GU)
                    for u in range(GU):
                        turned(i, first, g5, u)
                        lagging(i, first, g5, u)
                    if end and not first:
                        norm_root(held(act, i - 1))
                iterations(act, GI, group)
                g5 = held(act, (n * GI + GI) * GU)
                if not fresh:
                    relu(False, g5, -1)
                if not end:
                    copy_pq(GI, False, g5, -2)
                    copy_pq(GI, False, g5, -1)
                if end:
                    norm_root(GI - 1)

            def edge(layer):
                def part_hi(g4, q):
                    act.wait_ge(s_add, g4 + (q + 1))
                    nc.scalar.activation(msg[:, q % 2, 0, :, :], rows[:, q // 2 % 2, q % 2 * H:q % 2 * H + H, :],
                                         ACT.Relu).then_inc(s_hi, 1)

                def part_mid(g4, q):
                    act.wait_ge(s_rest, g4 + (q + 1))
                    nc.scalar.copy(msg[:, q % 2, 1, :, :], rows[:, q // 2 % 2, q % 2 * H:q % 2 * H + H, :]
                                   ).then_inc(s_mid, 1)

                def halves(i, first):
                    g = held(act, layer * ITERS + i)
                    g16, g4 = held(act, g * 16), held(act, g * 4)
                    for q in range(4):
                        lag = not (first and q == 0)
                        for k in range(4):
                            if k == 0 and lag:
                                part_hi(g4, q - 1)
                            if k == 2 and lag:
                                part_mid(g4, q - 1)
                            p = 4 * q + k
                            act.wait_ge(s_t, g16 + (p + 1))
                            if not first or p >= 2:
                                act.wait_ge(s_pre, g16 + (p - 1))
                            nc.scalar.copy(hot_t[:, p % 2, :, :].rearrange("p a b -> p (a b)"), t_bank(p)
                                           ).then_inc(s_tc, 1)
                iterations(act, ITERS, halves)
                g4 = held(act, layer * (4 * ITERS) + 4 * ITERS)
                part_hi(g4, -1)
                part_mid(g4, -1)

            phases(act, node, edge)

        @block.tensor
        def _(pe):
            pe.wait_ge(s_const, 1)

            def turn0(i32, c, *pairs):
                for k in pairs:
                    p = 8 * c + k
                    pe.wait_ge(s_hot0, i32 + (2 * p + 2))
                    for tt in range(2):
                        for j in range(2):
                            last = nc.tensor.transpose(
                                t_bank(p)[:, tt * 256 + j * PART:tt * 256 + (j + 1) * PART],
                                hot[:, (2 * p + tt) % (2 * K), j * PART:(j + 1) * PART], ident_b[:, :])
                    last.then_inc(s_t0, 1)

            def er0(i16, i2, c, *pairs):
                for k in pairs:
                    p = 8 * c + k
                    if k == 0:
                        pe.wait_ge(s_win, i2 + (c + 1))
                        if not (isinstance(i2, int) and i2 + c < 2):
                            pe.wait_ge(s_ec, i2 + (c - 1))
                    pe.wait_ge(s_tc0, i16 + (p + 1))
                    for tt in range(2):
                        for j in range(2):
                            last = nc.tensor.matmul(
                                er_bank(c % 2)[:, 2 * k + tt, :], hot_t[:, p % 2, tt, j * PART:(j + 1) * PART],
                                er_win[:, c % 2, 2 * k + tt, 3 * j:3 * j + 3], start=(j == 0), stop=(j == 1))
                    last.then_inc(s_er, 1)

            def sums0(i32, i2, c, lo, hi, start=False):
                if lo == 0:
                    pe.wait_ge(s_wlo, i2 + (c + 1))
                for t in range(lo, hi):
                    tau = K * c + t
                    if t % 2 == 0 and not (start and t < 4):
                        pe.wait_ge(s_acc0, i32 + (tau - 2))
                    for j in range(2):
                        for s in range(3):
                            last = nc.tensor.matmul(
                                agg_slot(tau)[:, j, 0:D + 1], hot[:, tau % (2 * K), j * PART:(j + 1) * PART],
                                wparts[:, c % 2, s, t, :], start=(s == 0), stop=(s == 2))
                    last.then_inc(s_aggm0, 1)

            def iter0(i, first):
                i32, i16, i2 = held(pe, i * 32), held(pe, i * 16), held(pe, i * 2)
                for b in range(2):
                    prev = not (first and b == 0)
                    start = first and b == 1
                    m = misc(b)
                    pe.wait_ge(s_ec, i2 + (b + 1))
                    nc.tensor.transpose(m["e_t"], ec[:, :], ident[:, :]).then_inc(s_et, 1)
                    pe.wait_ge(s_ends, i2 + (b + 1))
                    hold_waits(pe, s_past[1])
                    nc.tensor.transpose(m["ends"][:, 0:K], fwd[:, PART - 1:PART], ident[0:K, 0:K])
                    nc.tensor.transpose(m["ends"][:, K:2 * K], bwd[:, 0:1], ident[0:K, 0:K]).then_inc(s_endst, 1)
                    if prev:
                        sums0(i32, i2, b - 1, 0, 4, start)
                    pe.wait_ge(s_carry, i2 + (b + 1))
                    hold_waits(pe, s_past[1])
                    nc.tensor.transpose(m["carry"][:, 0:1], carry_row[:, 0:K], ident[0:1, 0:1])
                    nc.tensor.transpose(m["carry"][:, 1:2], carry_row[:, K:2 * K], ident[0:1, 0:1]
                                        ).then_inc(s_carryt, 1)
                    if prev:
                        sums0(i32, i2, b - 1, 4, 8)
                    turn0(i32, b + 1, 0, 1)
                    if prev:
                        sums0(i32, i2, b - 1, 8, 10)
                    er0(i16, i2, b + 1, 0, 1)
                    if prev:
                        sums0(i32, i2, b - 1, 10, 12)
                    turn0(i32, b + 1, 2, 3)
                    if prev:
                        sums0(i32, i2, b - 1, 12, 16)
                    er0(i16, i2, b + 1, 2, 3)
                    turn0(i32, b + 1, 4, 5)
                    pe.wait_ge(s_w, i2 + (b + 1))
                    hold_waits(pe, s_past[1])
                    nc.tensor.transpose(m["w_t"], w_row[:, :], ident[0:K, 0:K])
                    pe.wait_ge(s_resc, i2 + (b + 1))
                    nc.tensor.matmul(m["resc"], ones[:, :], resc[:, 1:2], start=True, stop=True
                                     ).then_inc(s_wt, 1)
                    er0(i16, i2, b + 1, 4, 5)
                    turn0(i32, b + 1, 6, 7)
                    er0(i16, i2, b + 1, 6, 7)

            for k in range(0, 8, 2):
                turn0(0, 0, k, k + 1)
                er0(0, 0, 0, k, k + 1)
            iterations(pe, ITERS, iter0)
            sums0(32 * ITERS, 2 * ITERS, -1, 0, K)

            def node(n):
                fresh = isinstance(n, int) and n == 0
                end = isinstance(n, int) and n == LAYERS
                pe.wait_ge(s_w_in, n * 64 + 64)
                if not fresh:
                    pe.wait_ge(s_keep, n * PH)

                def turn(first, g5, u):
                    pe.wait_ge(s_st, g5 + (u + 1))
                    if u == 0 and not first:
                        pe.wait_ge(s_rl if fresh else s_ca, g5 if fresh else g5 - PH)
                    if fresh and u >= 2:
                        pe.wait_ge(s_rl, g5 + (u - 1))
                    hold_waits(pe, s_past[1])
                    for k in range(GB):
                        last = nc.tensor.transpose(ps[0:D, u % 2, k * PART:(k + 1) * PART],
                                                   stage[:, u, k, :], ident[:, :])
                    last.then_inc(s_tr, 1)

                def update(i, first, g5, e):
                    u = e % GU
                    pe.wait_ge(s_ca, g5 + (e + 1) - PH)
                    if u == 0 and not first:
                        pe.wait_ge(s_rl, g5 + e)
                    if u >= 2:
                        pe.wait_ge(s_rl, g5 + (e - 1))
                    hold_waits(pe, s_past[1])
                    nc.tensor.matmul(ps[0:D, 2 + u % 2, :], w_u_sb[:, :],
                                     xs_t[:, ds((i * GU + e) * (GB * PART), GB * PART)],
                                     start=True, stop=True).then_inc(s_up, 1)

                def make_pq(first, g5, e):
                    u = e % GU
                    pe.wait_ge(s_rl, g5 + (e + 1))
                    if u == 0 and not first:
                        pe.wait_ge(s_qc, g5 + e)
                    if u == 4:
                        pe.wait_ge(s_qc, g5 + (e - 3))
                    hold_waits(pe, s_past[1])
                    for k in range(GB):
                        last = nc.tensor.matmul(ps[:, 4 + u % 4, k * 2 * D:(k + 1) * 2 * D],
                                                x_t[:, u, k * PART:(k + 1) * PART], w_ij_sb[:, :],
                                                start=True, stop=True)
                    last.then_inc(s_pq, 1)

                def turn_back(i, first, g5, e):
                    u = e % GU
                    pe.wait_ge(s_rl, g5 + (e + 1))
                    if u == 0 and not first:
                        pe.wait_ge(s_fin, i * GU + e)
                    if u == 4:
                        pe.wait_ge(s_fin, i * GU + (e - 3))
                    hold_waits(pe, s_past[1])
                    for k in range(GB):
                        last = nc.tensor.transpose(ps[:, 4 + u % 4, k * D:(k + 1) * D],
                                                   x_t[:, u, k * PART:(k + 1) * PART], ident[0:D, 0:D])
                    last.then_inc(s_back, 1)

                def onward(i, first, g5, e):
                    turn_back(i, first, g5, e) if end else make_pq(first, g5, e)

                def group(i, first):
                    g5 = held(pe, (n * GI + i) * GU)
                    for u in range(GU):
                        turn(first, g5, u)
                        if not fresh and not (first and u < 1):
                            update(i, first, g5, u - 1)
                        if not (first and u < 2):
                            onward(i, first, g5, u - 2)
                iterations(pe, GI, group)
                g5 = held(pe, (n * GI + GI) * GU)
                if not fresh:
                    update(GI, False, g5, -1)
                onward(GI, False, g5, -2)
                onward(GI, False, g5, -1)

            def edge(layer):
                def sums(g, g32, q, lo, hi, start=False):
                    if lo == 0:
                        pe.wait_ge(s_lo[q % 4], g + (q // 4 + 1))
                    for t in range(lo, hi):
                        tau = H * q + t
                        if t % 2 == 0 and not (start and t < 4):
                            pe.wait_ge(s_acc, g32 + (tau - 2))
                        for j in range(2):
                            for s in range(3):
                                last = nc.tensor.matmul(
                                    agg_slot(tau)[:, j, 0:D], hot[:, tau % (2 * K), j * PART:(j + 1) * PART],
                                    msg[:, q % 2, s, t, :], start=(s == 0), stop=(s == 2))
                        last.then_inc(s_aggm, 1)

                def halves(i, first):
                    g = held(pe, layer * ITERS + i)
                    g32, g16, g4 = held(pe, g * 32), held(pe, g * 16), held(pe, g * 4)
                    hb = held(pe, layer * (TILES + H) + i * 32)
                    for q in range(4):
                        b, h = q // 2, q % 2

                        def turn(p):
                            pe.wait_ge(s_hot, hb + (2 * p + 2))
                            for tt in range(2):
                                for j in range(2):
                                    last = nc.tensor.transpose(
                                        t_bank(p)[:, tt * 256 + j * PART:tt * 256 + (j + 1) * PART],
                                        hot[:, 2 * p + tt, j * PART:(j + 1) * PART], ident_b[:, :])
                            last.then_inc(s_t, 1)

                        turn(4 * q)
                        for k in range(4):
                            p = 4 * q + k
                            if k < 3:
                                turn(p + 1)
                            if not first or q >= 2:
                                sums(g, g32, q - 2, 2 * k, 2 * k + 2, start=first and q == 2)
                            if k == 0 and h == 0:
                                pe.wait_ge(s_edge[b], g * 16 + 16)
                            if k == 0 and (not first or q >= 2):
                                pe.wait_ge(s_add, g4 + (q - 1))
                            pe.wait_ge(s_tc, g16 + (p + 1))
                            for tt in range(2):
                                t = 2 * k + tt
                                o = pre_bank(q)[:, t, :]
                                for s in range(3):
                                    nc.tensor.matmul(o, edge_f[0:KE, b, h * H + t, :], w_e3[0:KE, s, :],
                                                     start=(s == 0), stop=False)
                                for j in range(2):
                                    for s in range(3):
                                        last = nc.tensor.matmul(
                                            o, hot_t[:, p % 2, tt, j * PART:(j + 1) * PART],
                                            win[:, H * (q % 2) + t, j * PW + s * D:j * PW + (s + 1) * D],
                                            start=False, stop=(j == 1 and s == 2))
                            last.then_inc(s_pre, 1)

                pe.wait_ge(s_we, layer * N_WE + N_WE)
                iterations(pe, ITERS, halves)
                g = held(pe, layer * ITERS + ITERS)
                g32 = held(pe, g * 32)
                sums(g, g32, -2, 0, H)
                sums(g, g32, -1, 0, H)

            phases(pe, node, edge)

        @block.vector
        def _(dve):
            v = nc.vector
            regs = [dve.alloc_register(f"tile_block{k}") for k in range(2 * K)]
            dve.sem_inc(s_p3, GU)
            pro = Chain(dve, s_pro)
            dve.wait_ge(s_iota, 1)
            v.memset(ones[:, :], 1.0)
            v.memset(zeros[:, :, :], 0.0)
            v.memset(eps[:, :], EPS)
            v.memset(fwd_chain[:, :, :], -BIG)
            v.memset(bwd_chain[:, :], -BIG)
            v.memset(agg_raw[:, :], 0.0)
            v.memset(agg1, 0.0)
            v.memset(rel[:, TILES:TILES + K], 0.0)
            v.memset(block_row[:, TILES:TILES + K], 0)
            v.memset(er[:, NB:NBP], 0.0)
            v.memset(xe[:, :, 0], 1.0)
            v.tensor_copy(pidx[:, :], pidx_i[:, :])
            pro.link(v.tensor_copy(iota[:, :], iota_i[:, :]))
            v.tensor_scalar(ident[:, :], iota[:, 0:PART], pidx[:, :], None, ALU.is_equal)
            v.tensor_scalar(ident_b[:, :], iota[:, 0:PART], pidx[:, :], None, ALU.is_equal)
            pro.link(v.tensor_scalar(resc_col[:, :], pidx[:, :], float(NREST), None, ALU.is_lt))
            for w in (al, ar):
                for h in range(2):
                    lo, hi = (0, NH) if h == 0 else (NH, NB)
                    prod = p3_raw[:, 0:(hi - lo) * D].rearrange("p (b d) -> p b d", d=D)
                    if w is al:
                        dve.wait_ge(s_xin[h], 16 * N_XIN)
                        if h == 1:
                            pro.link(v.tensor_scalar(xn[:, NT, :], xn[:, NT, :], resc_col[:, :], None, ALU.mult))
                    pro.link(v.tensor_tensor(prod, xn[:, lo:hi, :],
                                             w[:, :].unsqueeze(1).to_broadcast([PART, hi - lo, D]), ALU.mult))
                    if w is al:
                        v.tensor_reduce(xe[:, lo:hi, D + 1], prod, AX.X, ALU.add).then_inc(s_el, 1)
                        dve.wait_ge(s_el, h + 1)
                    else:
                        pro.link(v.tensor_reduce(er[:, lo:hi], prod, AX.X, ALU.add))
            dve.wait_ge(s_in, 16 * N_IN)
            pro.link(v.tensor_scalar(block_row[:, 0:TILES], first_i, 7, None, ALU.arith_shift_right))
            pro.link(v.tensor_scalar(first_b_i, first_b_i, 7, 7, ALU.arith_shift_right, ALU.logical_shift_left))
            pro.link(v.tensor_tensor(rel[:, 0:TILES], dst_c_i, first_b_i, ALU.subtract))
            one, cont, chain_f, chain_b = (flags[:, k, :] for k in range(4))
            pro.link(v.memset(flags[:, :, :], 0.0))
            v.tensor_tensor(one[:, 0:TILES], first_i, last_i, ALU.is_equal)
            pro.link(v.tensor_tensor(cont[:, 1:TILES], first_i[:, 1:TILES], last_i[:, 0:TILES - 1], ALU.is_equal))
            v.tensor_tensor(chain_f[:, 0:TILES], one[:, 0:TILES], cont[:, 0:TILES], ALU.mult)
            pro.link(v.tensor_tensor(chain_b[:, 0:TILES], one[:, 0:TILES], cont[:, 1:TILES + 1], ALU.mult))
            pro.link(v.tensor_scalar(flags[:, 1:4, :], flags[:, 1:4, :], 2 * BIG, -BIG, ALU.mult, ALU.add))
            pro.link(v.tensor_copy(er3[:, :, 0], er[:, :]))
            pro.link(v.tensor_tensor(er_rest[:, :], er[:, :], er3[:, :, 0], ALU.subtract))
            pro.link(v.tensor_copy(er3[:, :, 1], er_rest[:, :]))
            v.tensor_tensor(er3[:, :, 2], er_rest[:, :], er3[:, :, 1], ALU.subtract).then_inc(s_const, 1)

            def one_hots0(b, lo, hi):
                for t in range(lo, hi):
                    v.tensor_scalar(hot[:, K * b + t, :], iota[:, :], relc[:, b, t:t + 1], None, ALU.is_equal
                                    ).then_inc(s_hot0, 1)

            def accumulate0(i32, c, at, lo, hi):
                for t in range(lo, hi):
                    if t % 2 == 0:
                        dve.wait_ge(s_aggm0, i32 + (K * c + t + 2))
                    if t >= 2:
                        dve.wait_ge(s_acc0, i32 + (K * c + t - 1))
                    a = (agg0, agg1)[t % 2][:, ds(at[t - lo], 2), :]
                    v.tensor_tensor(a, a, agg_slot(K * c + t)[:, :, 0:D + 1], ALU.add).then_inc(s_acc0, 1)

            def part_rest(i2, c):
                dve.wait_ge(s_whi, i2 + (c + 1))
                v.tensor_tensor(weighted[:, :, :], weighted[:, :, :], wparts[:, c % 2, 0, :, :], ALU.subtract
                                ).then_inc(s_wrest, 1)

            def part_lo(i2, c):
                dve.wait_ge(s_wmid, i2 + (c + 1))
                v.tensor_tensor(wparts[:, c % 2, 2, :, :], weighted[:, :, :], wparts[:, c % 2, 1, :, :], ALU.subtract
                                ).then_inc(s_wlo, 1)

            def edge_lo(i2, c):
                dve.wait_ge(s_emid, i2 + (c + 1))
                v.tensor_tensor(e_out[:, c % 2, 2, :], e_rest[:, c % 2, :], e_out[:, c % 2, 1, :], ALU.subtract
                                ).then_inc(s_elo, 1)

            def iter0(i, first):
                i32, i16, i2 = held(dve, i * 32), held(dve, i * 16), held(dve, i * 2)
                ch = Chain(dve, s_ch0, held(dve, i * CH0))
                for b in range(2):
                    prev = not (first and b == 0)

                    ch.mark(v.tensor_copy(relc[:, 1 - b, :], rel[:, ds((i * 2 + b + 1) * K, K)]))
                    dve.wait_ge(s_dstrow[b], i16 + 16)
                    ch.link(v.tensor_tensor(same[:, :], dst_row[:, b, 1:PART + 2], dst_row[:, b, 0:PART + 1],
                                            ALU.is_equal))
                    ch.mark(v.tensor_scalar(same[:, :], same[:, :], 2 * BIG, -BIG, ALU.mult, ALU.add))
                    dve.wait_ge(s_fh, i2 + (b + 1))
                    ch.mark(v.tensor_scalar(resc_col[:, :], first_hot[:, b:b + 1], -1.0, 1.0, ALU.mult, ALU.add))
                    if prev:
                        edge_lo(i2, b - 1)
                    dve.wait_ge(s_rows0[b], i * (16 * K) + 16 * K)
                    dve.wait_ge(s_er, i16 + (8 * b + 8))
                    ch.link(v.tensor_reduce(ere[:, :], er_bank(b), AX.X, ALU.add))
                    ch.link(v.tensor_tensor(ere[:, :], ere[:, :], rows0[:, b, :, D + 1], ALU.add))
                    v.scalar_tensor_tensor(ec[:, :], ere[:, :], SLOPE, ere[:, :], ALU.mult, ALU.max
                                           ).then_inc(s_ec, 1)
                    if prev:
                        part_rest(i2, b - 1)
                        blocks = load_blocks(dve, regs, block_row, (i * 2 + b - 1) * K, K)

                    def fill(k):
                        for t in range(4 * k, 4 * k + 4):
                            if prev:
                                accumulate0(i32, b - 1, blocks[t:], t, t + 1)
                            one_hots0(1 - b, t, t + 1)

                    dve.wait_ge(s_et, i2 + (b + 1))
                    ch.link(v.tensor_copy(e_row[:, :], misc(b)["e_t"]))
                    v.tensor_tensor_scan(fwd[:, :], same[:, 0:PART], e_row[:, :], -BIG, ALU.min, ALU.max)
                    v.tensor_tensor_scan(bwd[:, ::-1], same[:, 1:PART + 1][:, ::-1], e_row[:, ::-1], -BIG,
                                         ALU.min, ALU.max).then_inc(s_ends, 1)
                    dve.wait_ge(s_ehi, i2 + (b + 1))
                    v.tensor_tensor(e_rest[:, b, :], e_in[:, b, :], e_out[:, b, 0, :], ALU.subtract
                                    ).then_inc(s_erest, 1)
                    if prev:
                        part_lo(i2, b - 1)
                    at = (i * 2 + b) * K
                    ch.mark(v.tensor_copy(carry_row[:, 0:K], chain_b[:, ds(at, K)]))
                    dve.wait_ge(s_endst, i2 + (b + 1))
                    ends = misc(b)["ends"]
                    ch.mark(v.tensor_tensor_scan(fwd_chain[:, b, 1:K + 1], chain_f[:, ds(at, K)], ends[:, 0:K],
                                                 fwd_chain[:, 1 - b, K:K + 1], ALU.min, ALU.max))
                    ch.join()
                    ch.mark(v.tensor_tensor_scan(bwd_chain[:, 0:K][:, ::-1], carry_row[:, 0:K][:, ::-1],
                                                 ends[:, K:2 * K][:, ::-1], -BIG, ALU.min, ALU.max))
                    ch.link(v.tensor_copy(fwd_chain[:, b, 0:1], fwd_chain[:, 1 - b, K:K + 1]))
                    v.tensor_tensor(carry_row[:, 0:K], cont[:, ds(at, K)], fwd_chain[:, b, 0:K], ALU.min)
                    v.tensor_tensor(carry_row[:, K:2 * K], cont[:, ds(at + 1, K)], bwd_chain[:, 1:K + 1], ALU.min
                                    ).then_inc(s_carry, 1)
                    fill(0)
                    fill(1)
                    dve.wait_ge(s_carryt, i2 + (b + 1))
                    ch.link(v.tensor_copy(carry_col[:, :], misc(b)["carry"]))
                    ch.mark(v.tensor_tensor_scan(fwd[:, :], same[:, 0:PART], e_row[:, :], carry_col[:, 0:1],
                                                 ALU.min, ALU.max))
                    ch.link(v.tensor_tensor_scan(bwd[:, ::-1], same[:, 1:PART + 1][:, ::-1], e_row[:, ::-1],
                                                 carry_col[:, 1:2], ALU.min, ALU.max))
                    ch.mark(v.tensor_scalar(resc[:, 1:2], same[0:1, 0:1], 0.0, 1.0 / BIG, ALU.max, ALU.mult))
                    ch.link(v.tensor_tensor(bwd[:, :], fwd[:, :], bwd[:, :], ALU.max))
                    v.tensor_tensor(shift[:, :], e_row[:, :], bwd[:, :], ALU.subtract).then_inc(s_shift, 1)
                    ch.mark(v.tensor_tensor(resc[:, 0:1], fwd_chain[:, b, 0:1], bwd[0:1, 0:1], ALU.subtract))
                    ch.join()
                    v.tensor_tensor(resc[:, 0:1], resc[:, 0:1], resc[:, 1:2], ALU.mult).then_inc(s_diff, 1)
                    fill(2)
                    fill(3)
                    dve.wait_ge(s_wt, i2 + (b + 1))
                    ch.mark(v.tensor_copy(w_col[:, :], misc(b)["w_t"]))
                    ch.link(v.scalar_tensor_tensor(resc_col[:, :], misc(b)["resc"], first_hot[:, b:b + 1],
                                                   resc_col[:, :], ALU.mult, ALU.add))
                    v.tensor_tensor(weighted[:, :, :], rows0[:, b, :, 0:D + 1],
                                    w_col[:, :].unsqueeze(2).to_broadcast([PART, K, D + 1]), ALU.mult
                                    ).then_inc(s_wf, 1)
                    blk = load_blocks(dve, regs, block_row, (i * 2 + b) * K, 1)[0]
                    if prev:
                        dve.wait_ge(s_acc0, i32 + K * b)
                    for a in (agg0[:, ds(blk, 1), :], agg1[:, ds(blk, 1), :]):
                        ch.mark(v.tensor_scalar(a, a, resc_col[:, :], None, ALU.mult))
                assert ch.n == CH0, ch.n

            ch = Chain(dve, s_pro, pro.n)
            ch.link(v.tensor_copy(relc[:, 0, :], rel[:, 0:K]))
            one_hots0(0, 0, K)
            iterations(dve, ITERS, iter0)
            edge_lo(2 * ITERS, -1)
            part_rest(2 * ITERS, -1)
            part_lo(2 * ITERS, -1)
            at = load_blocks(dve, regs, block_row, TILES - K, K)
            accumulate0(32 * ITERS, -1, at, 0, K)
            dve.wait_ge(s_acc0, TILES)

            ln = Chain(dve, s_ln)

            def bc(a):
                return a.unsqueeze(2).to_broadcast([PART, NB, D])

            def layernorm(y, z, o):
                ln.link(v.tensor_reduce(stat[:, 0, 0:NB], y, AX.X, ALU.add))
                ln.link(v.tensor_scalar(stat[:, 0, 0:NB], stat[:, 0, 0:NB], 1.0 / D, None, ALU.mult))
                ln.link(v.tensor_tensor(y, y, bc(stat[:, 0, 0:NB]), ALU.subtract))
                ln.link(v.tensor_tensor(z, y, y, ALU.mult))
                ln.link(v.tensor_reduce(stat[:, 1, 0:NB], z, AX.X, ALU.add))
                dve.wait_ge(s_lna, 2)
                ln.link(v.reciprocal(stat[:, 3, 0:NB], stat[:, 2, 0:NB]))
                v.tensor_tensor(o, y, bc(stat[:, 3, 0:NB]), ALU.mult).then_inc(s_x1, 1)

            ln.link(v.tensor_tensor(agg0[:, 0:NB, :], agg0[:, 0:NB, :], agg1[:, 0:NB, :], ALU.add))
            ln.link(v.tensor_scalar(stat[:, 0, 0:NB], agg0[:, 0:NB, 0], 1e-30, None, ALU.max))
            ln.link(v.reciprocal(stat[:, 1, 0:NB], stat[:, 0, 0:NB]))
            ln.link(v.tensor_tensor(bulk_a, agg0[:, 0:NB, 1:D + 1], bc(stat[:, 1, 0:NB]), ALU.mult))
            ln.link(v.tensor_scalar(bulk_b, bulk_a, 0.0, None, ALU.min))
            ln.link(v.scalar_tensor_tensor(bulk_a, bulk_a, 0.0, xn, ALU.max, ALU.add))
            dve.wait_ge(s_lna, 1)
            ln.link(v.scalar_tensor_tensor(bulk_a, bulk_b, -1.0, bulk_a, ALU.add, ALU.add))
            v.memset(agg[:, NB:NBP, :], 0.0)
            for s in range(2):
                dve.wait_ge(s_eout[s], 16 * ITERS)
            layernorm(bulk_a, bulk_b, agg[:, 0:NB, :])
            dve.wait_ge(s_x1, 1)

            def node(n):
                end = isinstance(n, int) and n == LAYERS
                if not end:
                    dve.wait_ge(s_w_in, n * 64 + 64)
                    we = Chain(dve, s_we, held(dve, n * N_WE))
                    part = [w_e_part[:, s, :] for s in range(3)]
                    we.link(v.tensor_copy(part[0], w_e_sb[:, :]))
                    we.link(v.tensor_tensor(w_e_rest[:, :], w_e_sb[:, :], part[0], ALU.subtract))
                    we.link(v.tensor_copy(part[1], w_e_rest[:, :]))
                    we.link(v.tensor_tensor(part[2], w_e_rest[:, :], part[1], ALU.subtract))
                    we.link(v.tensor_scalar(w_e_rest[:, :], part[0], mask[:, 0:1], None, ALU.mult))
                    we.link(v.scalar_tensor_tensor(w_e_rest[:, :], part[1], mask[:, 1:2], w_e_rest[:, :],
                                                   ALU.mult, ALU.add))
                    we.mark(v.scalar_tensor_tensor(w_e3[:, 0, :], part[2], mask[:, 2:3], w_e_rest[:, :],
                                                   ALU.mult, ALU.add))
                    we.mark(v.tensor_scalar(w_e3[:, 1, :], part[1], mask[:, 3:4], None, ALU.mult))
                    we.link(v.tensor_scalar(w_e3[:, 2, :], part[2], mask[:, 3:4], None, ALU.mult))
                    assert we.n == N_WE
                else:
                    v.memset(p3_raw[:, NB * D:NBP * D], 0.0)
                    dve.wait_ge(s_x1d, 32)

                def split(i, g5, g15, u):
                    dve.wait_ge(s_qc, g5 + (u + 1))
                    p_f = stage_pq[:, u, :, 0:D]
                    at = (i * GU + u) * GB
                    part = [p3[:, ds(at * PW, GB * PW)].rearrange("p (b w) -> p b w", w=PW)[:, :, s * D:(s + 1) * D]
                            for s in range(3)]
                    v.tensor_copy(part[0], p_f).then_inc(s_split, 1)
                    dve.wait_ge(s_split, g15 + (3 * u + 1))
                    v.tensor_tensor(p_rest[:, :, :], p_f, part[0], ALU.subtract).then_inc(s_split, 1)
                    dve.wait_ge(s_split, g15 + (3 * u + 2))
                    v.tensor_copy(part[1], p_rest[:, :, :]).then_inc(s_split, 1)
                    dve.wait_ge(s_split, g15 + (3 * u + 3))
                    v.tensor_tensor(part[2], p_rest[:, :, :], part[1], ALU.subtract).then_inc(s_p3, 1)

                def add_back(i, u):
                    dve.wait_ge(s_back, held(dve, i * GU) + (u + 1))
                    y = p3_raw[:, ds((i * GU + u) * (GB * D), GB * D)]
                    v.tensor_tensor(y, y, ps[:, 4 + u % 4, 0:GB * D], ALU.add).then_inc(s_fin, 1)

                def norm(i):
                    nb = GU * GB
                    nm = Chain(dve, s_nm, held(dve, i * N_NM))

                    def over(a):
                        return a.unsqueeze(2).to_broadcast([PART, nb, D])

                    y = p3_raw[:, ds(i * (nb * D), nb * D)].rearrange("p (b d) -> p b d", d=D)
                    z = shared[:, n_st:2 * n_st].rearrange("p (b d) -> p b d", d=D)
                    dve.wait_ge(s_fin, held(dve, i * GU) + GU)
                    nm.link(v.tensor_reduce(stat[:, 0, 0:nb], y, AX.X, ALU.add))
                    nm.link(v.tensor_scalar(stat[:, 0, 0:nb], stat[:, 0, 0:nb], 1.0 / D, None, ALU.mult))
                    nm.link(v.tensor_tensor(y, y, over(stat[:, 0, 0:nb]), ALU.subtract))
                    nm.link(v.tensor_tensor(z, y, y, ALU.mult))
                    nm.link(v.tensor_reduce(stat[:, 1, 0:nb], z, AX.X, ALU.add))
                    dve.wait_ge(s_nma, held(dve, i) + 1)
                    nm.link(v.reciprocal(stat[:, 3, 0:nb], stat[:, 2, 0:nb]))
                    assert nm.n == N_NM
                    v.tensor_tensor(agg[:, ds(i * nb, nb), :], y, over(stat[:, 3, 0:nb]), ALU.mult
                                    ).then_inc(s_res, 1)

                def finish(i, u, g5, g15):
                    add_back(i, u) if end else split(i, g5, g15, u)

                def group(i, first):
                    if not first:
                        before = held(dve, i - 1)
                        g5 = held(dve, (n * GI + before) * GU)
                        g15 = held(dve, g5 * 3)
                    for u in range(GU):
                        if not first:
                            dve.wait_ge(s_tr, g5 + (u + 1))
                        v.tensor_copy(stage[:, u, :, :], agg[:, ds((i * GU + u) * GB, GB), :]).then_inc(s_st, 1)
                        if not first:
                            finish(before, u, g5, g15)
                    if end and not first:
                        norm(before)
                iterations(dve, GI, group)
                g5 = held(dve, (n * GI + (GI - 1)) * GU)
                g15 = held(dve, g5 * 3)
                for u in range(GU):
                    finish(GI - 1, u, g5, g15)
                if end:
                    norm(GI - 1)

            def edge(layer):
                def take(c, g2, i):
                    v.tensor_copy(relc[:, c % 2, :], rel[:, ds((i * 2 + c) * K, K)]).then_inc(s_relc, 1)
                    dve.wait_ge(s_relc, g2 + (c + 1))

                def prepare(q, at, lo, hi):
                    b, h = q // 2 % 2, q % 2
                    for t in range(lo, hi):
                        c = h * H + t
                        v.tensor_copy(win[:, H * h + t, :], p3[:, ds(at[t] * PW, 2 * PW)])
                        v.tensor_scalar(hot[:, K * b + c, :], iota[:, :], relc[:, b, c:c + 1], None,
                                        ALU.is_equal).then_inc(s_hot, 1)

                def accumulate(g32, q, at, lo, hi, start=False):
                    for t in range(lo, hi):
                        tau = H * q + t
                        if t % 2 == 0:
                            dve.wait_ge(s_aggm, g32 + (tau + 2))
                        if not (start and t == 0):
                            dve.wait_ge(s_acc, g32 + tau)
                        a = agg[:, ds(at[t], 2), :]
                        v.tensor_tensor(a, a, agg_slot(tau)[:, :, 0:D], ALU.add).then_inc(s_acc, 1)

                def rest(g4, q):
                    m = rows[:, q // 2 % 2, q % 2 * H:q % 2 * H + H, :]
                    dve.wait_ge(s_hi, g4 + (q + 1))
                    v.scalar_tensor_tensor(m, m, 0.0, msg[:, q % 2, 0, :, :], ALU.max, ALU.subtract
                                           ).then_inc(s_rest, 1)

                def low(g4, q):
                    m = rows[:, q // 2 % 2, q % 2 * H:q % 2 * H + H, :]
                    dve.wait_ge(s_mid, g4 + (q + 1))
                    v.tensor_tensor(msg[:, q % 2, 2, :, :], m, msg[:, q % 2, 1, :, :], ALU.subtract
                                    ).then_inc(s_lo[q % 4], 1)

                def halves(i, first):
                    g = held(dve, layer * ITERS + i)
                    g32, g16, g4 = held(dve, g * 32), held(dve, g * 16), held(dve, g * 4)
                    r2 = held(dve, layer * (2 * ITERS + 1) + i * 2)
                    for q in range(4):
                        b, h = q // 2, q % 2
                        lag1, lag2 = not (first and q == 0), not (first and q < 2)
                        nxt = load_blocks(dve, regs[:H], block_row, (i * 4 + q + 1) * H, H)
                        if lag2:
                            old = load_blocks(dve, regs[K:K + H], block_row, (i * 4 + q - 2) * H, H)
                        if h == 1:
                            take(b + 1, r2, i)
                        for t in range(H):
                            if t == 1 and lag1:
                                rest(g4, q - 1)
                            if t == 5 and lag1:
                                low(g4, q - 1)
                            if lag2:
                                accumulate(g32, q - 2, old, t, t + 1, start=first and q == 2)
                            prepare(q + 1, nxt, t, t + 1)
                        dve.wait_ge(s_pre, g16 + 4 * (q + 1))
                        dve.wait_ge(s_rows[b][h], g * 128 + 128)
                        m = rows[:, b, h * H:h * H + H, :]
                        v.tensor_tensor(m, m, pre_bank(q), ALU.add).then_inc(s_add, 1)

                for u in range(GU):
                    dve.wait_ge(s_qt[u], layer * (16 * GI) + 16 * (GI + 1))
                dve.wait_ge(s_zero, layer * PH + PH)
                hold_waits(dve, s_past[2])
                nxt = load_blocks(dve, regs[:H], block_row, 0, H)
                take(0, held(dve, layer * (2 * ITERS + 1)), 0)
                prepare(0, nxt, 0, H)
                iterations(dve, ITERS, halves)
                g4 = held(dve, layer * (4 * ITERS) + 4 * ITERS)
                g32 = held(dve, layer * TILES + TILES)
                rest(g4, -1)
                low(g4, -1)
                for q in (-2, -1):
                    old = load_blocks(dve, regs[K:K + H], block_row, TILES + q * H, H)
                    accumulate(g32, q, old, 0, H)
                dve.wait_ge(s_acc, g32)

            phases(dve, node, edge)


def dst_rows(dst_flat, at):
    row = dst_flat[0:1, bass.ds(at, K * PART + 2)]
    return bass.AP(tensor=row.tensor, offset=row.offset, ap=[[PART, K], [1, PART + 2]])


def hold_waits(engine, past):
    engine.sem_inc(past, 1)


def load_blocks(engine, regs, block_row, at, n):
    engine.load(regs[:n], block_row[0:1, bass.ds(at, n)])
    return [engine.snap(r, min_val=0, max_val=NB - 1) for r in regs[:n]]


_OUT = ((N, D), "float32")


def kernel(x, src, dst, edge_attr_16, L0_gnn_attn_l, L0_gnn_attn_r, L1_gnn_msg_w, L1_gnn_msg_b,
           L1_gnn_upd_w, L1_gnn_upd_b):
    import concourse.bacc as bacc
    from concourse.bass_utils import run_bass_kernel_spmd

    src, dst, ef = np.asarray(src), np.asarray(dst), np.asarray(edge_attr_16)
    pad = TILES * PART - E
    src_p = np.concatenate([src, np.zeros(pad, src.dtype)])
    dst_p = np.concatenate([dst, np.full(pad, NB * PART - 1, dst.dtype)])
    tiles = dst_p.reshape(TILES, PART)
    mw, uw = np.asarray(L1_gnn_msg_w), np.asarray(L1_gnn_upd_w)
    mb, ub = np.asarray(L1_gnn_msg_b), np.asarray(L1_gnn_upd_b)
    none = np.zeros((1, PART, D), mw.dtype)
    w_e = np.zeros((LAYERS, WR, D), mw.dtype)
    w_e[:, 0:3 * DE] = np.tile(mw[:, 2 * D:], (1, 3, 1))
    w_e[:, 3 * DE:KE] = mb[:, None]
    masks = np.zeros((WR, 4), np.float32)
    masks[0:3 * DE, [0, 3]] = 1
    for part in range(3):
        masks[3 * DE + part, part] = 1
    arrays = {
        "x": np.asarray(x),
        "src_cols": src_p.reshape(TILES, PART).T,
        "dst_cols": tiles.T,
        "dst_flat": np.concatenate([np.full(1, -1, dst.dtype), dst_p, np.full(1, -1, dst.dtype)])[None],
        "dst_first": tiles[:, 0][None],
        "dst_last": tiles[:, -1][None],
        "edge_t": np.concatenate([ef, np.zeros((pad, DE), ef.dtype)]).T,
        "attn_l": np.asarray(L0_gnn_attn_l)[None],
        "attn_r": np.asarray(L0_gnn_attn_r)[None],
        "w_ij": np.concatenate([np.concatenate([mw[:, 0:D], mw[:, D:2 * D]], axis=2), none[:, 0:D].repeat(2, 2)]
                               ).reshape((LAYERS + 1) * D, 2 * D),
        "w_e": np.concatenate([w_e, none[:, 0:WR]]).reshape((LAYERS + 1) * WR, D),
        "w_u": np.concatenate([none, uw]).reshape((LAYERS + 1) * PART, D),
        "b_u": np.concatenate([np.zeros((1, D), ub.dtype), ub]).reshape((LAYERS + 1) * D, 1),
        "masks": masks,
    }
    arrays = {k: np.ascontiguousarray(a) for k, a in arrays.items()}
    nc = bacc.Bacc("TRN2", target_bir_lowering=False, num_devices=1)
    args = {k: nc.dram_tensor(f"in_{k}", a.shape, mybir.dt.from_np(a.dtype), kind="ExternalInput").ap()
            for k, a in arrays.items()}
    out = nc.dram_tensor("out_0", _OUT[0], F32, kind="ExternalOutput").ap()
    build(nc, out=out, **args)
    result = run_bass_kernel_spmd(nc, [{f"in_{k}": a for k, a in arrays.items()}], core_ids=[0])
    return result.results[0]["out_0"]
```
